# Optimizing a Trainium2 kernel written in Bass

```python
import numpy as np
import jax
import jax.numpy as jnp

def _softmax(x, axis=-1):
    return jax.nn.softmax(x, axis=axis)

def _gelu(x):
    return jax.nn.gelu(x, approximate=True)

def _silu(x):
    return jax.nn.silu(x)

def _sigmoid(x):
    return jax.nn.sigmoid(x)

def _layernorm(x, axis=-1, eps=1e-05):
    m = jnp.mean(x, axis=axis, keepdims=True)
    v = jnp.var(x, axis=axis, keepdims=True)
    return (x - m) / jnp.sqrt(v + eps)

def _scatter_add(tgt, idx, src, axis=0):
    return tgt.at[idx].add(src)

def _segment_sum(src, seg, n):
    return jax.ops.segment_sum(src, seg, n)
kernel_name = 'mk_adaln_d1_jaxref_r4_3fa73c'

def setup_inputs(seed: int=0):
    np.random.seed(seed)
    _w = jnp.asarray

    def _L0_attn_setup():
        import jax, jax.numpy as jnp
        import numpy as np
        import math
        D_MODEL, N_HEADS, D_K, D_C, D_HR = (256, 8, 128, 32, 32)
        B, S = (4, 512)
        key = jax.random.key(seed)
        ks = jax.random.split(key, 17)

        def lin(k, fan_in, fan_out):
            lim = 1.0 / math.sqrt(fan_in)
            kw, kb = jax.random.split(k)
            W = jax.random.uniform(kw, (fan_in, fan_out), jnp.float32, -lim, lim)
            b = jax.random.uniform(kb, (fan_out,), jnp.float32, -lim, lim)
            return (W, b)
        W_DQ, b_DQ = lin(ks[0], D_MODEL, D_C)
        W_UQ, b_UQ = lin(ks[1], D_C, N_HEADS * D_K)
        W_DKV, b_DKV = lin(ks[2], D_MODEL, D_C)
        W_UK, b_UK = lin(ks[3], D_C, N_HEADS * D_K)
        W_UV, b_UV = lin(ks[4], D_C, N_HEADS * D_K)
        W_QR, b_QR = lin(ks[5], D_C, N_HEADS * D_HR)
        W_KR, b_KR = lin(ks[6], D_MODEL, D_HR)
        W_O, b_O = lin(ks[7], N_HEADS * D_K, D_MODEL)
        h_t = jax.random.normal(ks[8], (B, S, D_MODEL), jnp.float32)
        return {'h_t': h_t, 'W_DQ': W_DQ, 'b_DQ': b_DQ, 'W_UQ': W_UQ, 'b_UQ': b_UQ, 'W_DKV': W_DKV, 'b_DKV': b_DKV, 'W_UK': W_UK, 'b_UK': b_UK, 'W_UV': W_UV, 'b_UV': b_UV, 'W_QR': W_QR, 'b_QR': b_QR, 'W_KR': W_KR, 'b_KR': b_KR, 'W_O': W_O, 'b_O': b_O}
    _L0_attn_in = _L0_attn_setup()

    def _L0_ffn_setup():
        import math
        import jax, jax.numpy as jnp
        import numpy as np
        NUM_EXPERTS = 8
        CAPACITY_FACTOR = 1.5
        key = jax.random.key(seed)
        ks = jax.random.split(key, 4)
        B, T, D, F, E = (4, 512, 256, 1024, NUM_EXPERTS)
        scale = 0.02
        return {'x': jax.random.normal(ks[0], (B, T, D), dtype=jnp.float32), 'router_w': jax.random.normal(ks[1], (E, D), dtype=jnp.float32) * scale, 'w1': jax.random.normal(ks[2], (E, D, F), dtype=jnp.float32) * scale, 'b1': jnp.zeros((E, F), dtype=jnp.float32), 'w2': jax.random.normal(ks[3], (E, F, D), dtype=jnp.float32) * scale, 'b2': jnp.zeros((E, D), dtype=jnp.float32)}
    _L0_ffn_in = _L0_ffn_setup()
    _L0_c = _w((lambda *s: np.random.randn(*s).astype(np.float32) * 0.05)(4, 256))
    _L0_wmod = _w((lambda *s: np.random.randn(*s).astype(np.float32) * 0.05)(256, 6 * 256) * 256 ** (-0.5))
    _d = {'L0_attn_h_t': _L0_attn_in['h_t'], 'L0_attn_W_DQ': _L0_attn_in['W_DQ'], 'L0_attn_b_DQ': _L0_attn_in['b_DQ'], 'L0_attn_W_UQ': _L0_attn_in['W_UQ'], 'L0_attn_b_UQ': _L0_attn_in['b_UQ'], 'L0_attn_W_DKV': _L0_attn_in['W_DKV'], 'L0_attn_b_DKV': _L0_attn_in['b_DKV'], 'L0_attn_W_UK': _L0_attn_in['W_UK'], 'L0_attn_b_UK': _L0_attn_in['b_UK'], 'L0_attn_W_UV': _L0_attn_in['W_UV'], 'L0_attn_b_UV': _L0_attn_in['b_UV'], 'L0_attn_W_QR': _L0_attn_in['W_QR'], 'L0_attn_b_QR': _L0_attn_in['b_QR'], 'L0_attn_W_KR': _L0_attn_in['W_KR'], 'L0_attn_b_KR': _L0_attn_in['b_KR'], 'L0_attn_W_O': _L0_attn_in['W_O'], 'L0_attn_b_O': _L0_attn_in['b_O'], 'L0_ffn_router_w': _L0_ffn_in['router_w'], 'L0_ffn_w1': _L0_ffn_in['w1'], 'L0_ffn_b1': _L0_ffn_in['b1'], 'L0_ffn_w2': _L0_ffn_in['w2'], 'L0_ffn_b2': _L0_ffn_in['b2'], 'L0_c': _L0_c, 'L0_wmod': _L0_wmod}
    _x0 = _d['L0_attn_h_t']
    _d['L0_attn_h_t'] = jax.random.normal(jax.random.fold_in(jax.random.key(seed), 1), (4, 1024, 256), dtype=_x0.dtype)
    del _x0
    return _d

def reference(L0_attn_h_t, L0_attn_W_DQ, L0_attn_b_DQ, L0_attn_W_UQ, L0_attn_b_UQ, L0_attn_W_DKV, L0_attn_b_DKV, L0_attn_W_UK, L0_attn_b_UK, L0_attn_W_UV, L0_attn_b_UV, L0_attn_W_QR, L0_attn_b_QR, L0_attn_W_KR, L0_attn_b_KR, L0_attn_W_O, L0_attn_b_O, L0_ffn_router_w, L0_ffn_w1, L0_ffn_b1, L0_ffn_w2, L0_ffn_b2, L0_c, L0_wmod):

    def _L0_attn_ref(h_t, W_DQ, b_DQ, W_UQ, b_UQ, W_DKV, b_DKV, W_UK, b_UK, W_UV, b_UV, W_QR, b_QR, W_KR, b_KR, W_O, b_O):
        import jax, jax.numpy as jnp
        import numpy as np
        import math
        D_MODEL, N_HEADS, D_K, D_C, D_HR = (256, 8, 128, 32, 32)
        B, S = (4, 512)
        b, s, _ = h_t.shape
        c_q = h_t @ W_DQ + b_DQ
        c_kv = h_t @ W_DKV + b_DKV
        q_c = (c_q @ W_UQ + b_UQ).reshape(b, s, N_HEADS, D_K).transpose(0, 2, 1, 3)
        k_c = (c_kv @ W_UK + b_UK).reshape(b, s, N_HEADS, D_K).transpose(0, 2, 1, 3)
        v_c = (c_kv @ W_UV + b_UV).reshape(b, s, N_HEADS, D_K).transpose(0, 2, 1, 3)
        q_r = (c_q @ W_QR + b_QR).reshape(b, s, N_HEADS, D_HR).transpose(0, 2, 1, 3)
        k_r = (h_t @ W_KR + b_KR)[:, None, :, :]
        k_r = jnp.broadcast_to(k_r, (b, N_HEADS, s, D_HR))
        q = jnp.concatenate([q_c, q_r], axis=-1)
        k = jnp.concatenate([k_c, k_r], axis=-1)
        scale = 1.0 / math.sqrt(D_K + D_HR)
        scores = jnp.einsum('bhsd,bhtd->bhst', q, k) * scale
        attn = jax.nn.softmax(scores, axis=-1)
        o = jnp.einsum('bhst,bhtd->bhsd', attn, v_c)
        o = o.transpose(0, 2, 1, 3).reshape(b, s, N_HEADS * D_K)
        return o @ W_O + b_O

    def _L0_ffn_ref(x, router_w, w1, b1, w2, b2):
        import math
        import jax, jax.numpy as jnp
        import numpy as np
        NUM_EXPERTS = 8
        CAPACITY_FACTOR = 1.5
        B, T, D = x.shape
        E = router_w.shape[0]
        N = B * T
        C = max(math.ceil(CAPACITY_FACTOR * N / E), 1)
        x_flat = x.reshape(N, D)
        logits = x_flat @ router_w.T
        probs = jax.nn.softmax(logits, axis=-1)
        chosen_e = jnp.argmax(probs, axis=-1)
        chosen_p = jnp.max(probs, axis=-1)
        onehot = jax.nn.one_hot(chosen_e, E, dtype=jnp.float32)
        pos = jnp.take_along_axis(jnp.cumsum(onehot, axis=0), chosen_e[:, None], axis=1)[:, 0] - 1.0
        pos = pos.astype(jnp.int32)
        kept = pos < C
        pos_c = jnp.clip(pos, 0, C - 1)
        buf = jnp.zeros((E, C, D), dtype=x.dtype).at[chosen_e, pos_c].add(x_flat * kept[:, None].astype(x.dtype))
        h = jax.nn.gelu(jnp.einsum('ecd,edf->ecf', buf, w1) + b1[:, None, :], approximate=False)
        eo = jnp.einsum('ecf,efd->ecd', h, w2) + b2[:, None, :]
        y = eo[chosen_e, pos_c] * (chosen_p * kept.astype(x.dtype))[:, None]
        return y.reshape(B, T, D)
    x = L0_attn_h_t
    mod = (_silu(L0_c) @ L0_wmod).reshape(L0_c.shape[0], 6, 1, -1)
    sa, ca, ga, sb, cb, gb = (mod[:, 0], mod[:, 1], mod[:, 2], mod[:, 3], mod[:, 4], mod[:, 5])
    ga = (2 * (ga >= 0) - 1) * jnp.maximum(jnp.abs(ga), 0.25)
    gb = (2 * (gb >= 0) - 1) * jnp.maximum(jnp.abs(gb), 0.25)
    h = _layernorm(x, axis=-1) * (1 + ca) + sa
    x = x + ga * _L0_attn_ref(h, L0_attn_W_DQ, L0_attn_b_DQ, L0_attn_W_UQ, L0_attn_b_UQ, L0_attn_W_DKV, L0_attn_b_DKV, L0_attn_W_UK, L0_attn_b_UK, L0_attn_W_UV, L0_attn_b_UV, L0_attn_W_QR, L0_attn_b_QR, L0_attn_W_KR, L0_attn_b_KR, L0_attn_W_O, L0_attn_b_O)
    h = _layernorm(x, axis=-1) * (1 + cb) + sb
    x = x + gb * _L0_ffn_ref(h, L0_ffn_router_w, L0_ffn_w1, L0_ffn_b1, L0_ffn_w2, L0_ffn_b2)
    return x

_drawn_inputs = setup_inputs


def setup_inputs(seed=0):
    import zlib

    import numpy as np

    out = dict(_drawn_inputs(seed))
    spreads = {'L0_ffn_b1': (0.0, 0.8), 'L0_ffn_b2': (0.0, 2.0)}
    factors = {'L0_attn_W_DQ': 8.0,
     'L0_attn_b_DQ': 8.0,
     'L0_attn_W_UQ': 8.0,
     'L0_attn_b_UQ': 8.0,
     'L0_attn_W_DKV': 8.0,
     'L0_attn_b_DKV': 8.0,
     'L0_attn_W_UK': 8.0,
     'L0_attn_b_UK': 64.0,
     'L0_attn_W_UV': 8.0,
     'L0_attn_b_UV': 12.696,
     'L0_attn_W_QR': 8.0,
     'L0_attn_b_QR': 8.0,
     'L0_attn_W_KR': 8.0,
     'L0_attn_b_KR': 64.0,
     'L0_attn_W_O': 3.673,
     'L0_attn_b_O': 64.0,
     'L0_ffn_router_w': 7.843,
     'L0_ffn_w1': 8.0,
     'L0_ffn_w2': 8.0,
     'L0_c': 3.267,
     'L0_wmod': 3.277}
    for name, (base, spread) in spreads.items():
        noise = np.random.default_rng([zlib.crc32(name.encode()), seed]).standard_normal(out[name].shape)
        drawn = base * np.exp(spread * noise) if base else spread * noise
        out[name] = jnp.asarray(drawn.astype(out[name].dtype))
    for name, factor in factors.items():
        out[name] = (out[name] * factor).astype(out[name].dtype)
    return out
```

```python
from contextlib import ExitStack

import numpy as np
import concourse.bass as bass
from concourse import mybir

fp32 = mybir.dt.float32
fp16 = mybir.dt.float16
i32 = mybir.dt.int32
u32 = mybir.dt.uint32
ALU = mybir.AluOpType
ACT = mybir.ActivationFunctionType
AX = mybir.AxisListType

P = 128
B, S, D = 4, 1024, 256
H, DK, DC, DR = 8, 128, 32, 32
E, F = 8, 1024
N = B * S
CAP = -(-3 * N // (2 * E))
KD = D // P
ST = S // P
NT = N // P
SLOTS = E * CAP
ET = CAP // P
FT = F // P
HALF = 512
LR = DC + DR
QROWS = 3 * DC + 2
SCALE = float(DK + DR) ** -0.5
EPS = 1e-5

ALL = tuple(range(8))
CAST_ACT = (0, 3, 6)
CAST_POOL = (1, 2, 4, 5, 7)
SUB_POOL = (1, 3, 5, 7)
SUB_DVE = (0, 2, 4, 6)


def count_after(events, head, k):
    return (head + 1) * len(events) + events.index(k) + 1


def adaln_block(nc, h_t, W_DQ, b_DQ, W_UQ, b_UQ, W_DKV, b_DKV, W_UK, b_UK, W_UV, b_UV, W_QR, b_QR,
                W_KR, b_KR, W_O, b_O, router_w, w1, b1, w2, b2, c, wmod, out):
    x_tiles = h_t.rearrange("b (t p) d -> p (b t) d", p=P)
    out_tiles = out.rearrange("b (t p) d -> p (b t) d", p=P)
    xbuf = nc.dram_tensor("xbuf", [SLOTS + P, D], fp32).ap()
    ybuf = nc.dram_tensor("ybuf", [SLOTS, D], fp32).ap()

    ctx = ExitStack()
    with ctx:
        def sem(name):
            return ctx.enter_context(nc.semaphore(name))

        def sb(scope, name, shape, dt=fp32):
            return scope.enter_context(nc.sbuf_tensor(name, shape, dt))

        def ps(scope, name, shape, dt=fp32):
            return scope.enter_context(nc.psum_tensor(name, shape, dt))

        ident = sb(ctx, "ident", [P, P])
        ident16 = sb(ctx, "ident16", [P, P], fp16)
        upto16 = sb(ctx, "upto16", [P, P], fp16)
        ones16 = sb(ctx, "ones16", [P, P], fp16)
        mod = sb(ctx, "mod", [P, B, 4, D])
        GA, SB_, CB, GB = range(4)
        proj = sb(ctx, "proj", [P, H // 2, D])
        attn_bias = sb(ctx, "attn_bias", [P, D])
        cols = sb(ctx, "cols", [P, 96])
        b1T = cols[:, 0:64].rearrange("p (e f) -> p e f", e=E)
        rwT = cols[:, 64:80].rearrange("p (e k) -> p k e", e=E)
        rev = sb(ctx, "rev", [P, E])
        first_slot = sb(ctx, "first_slot", [P, E])
        trash = sb(ctx, "trash", [P, 1])
        minus_half = sb(ctx, "minus_half", [P, ST])
        x1 = sb(ctx, "x1", [P, NT, D])
        slot_of = sb(ctx, "slot_of", [P, NT], u32)
        gate_of = sb(ctx, "gate_of", [P, NT])

        loads = sem("loads")
        zeroed = sem("zeroed")

        const_v = sem("const_v")

        def wait_apart(eng, *waits):
            waits = [(sm, value if isinstance(value, int) else eng.compute_val(value)) for sm, value in waits]
            eng.wait_ge(const_v, 1)
            for sm, value in waits:
                eng.wait_ge(sm, value)

        inner = ExitStack()
        KA = sb(inner, "KA", [P, N], fp16)
        KB = sb(inner, "KB", [LR + 2, N], fp16)
        CQ = sb(inner, "CQ", [QROWS, N], fp16)
        VV = sb(inner, "VV", [P, NT, P], fp16)
        GQ = sb(inner, "GQ", [QROWS, H, P], fp16)
        mz = sb(inner, "mz", [P, ST, LR + 2], fp16)
        raw = sb(inner, "raw", [P, S])
        rinv = sb(inner, "rinv", [2 * DC, S])

        one = ExitStack()
        xs = x1
        wk = sb(one, "wk", [P, KD, P])
        wq = sb(one, "wq", [P, KD, 3 * DC])
        bk = sb(one, "bk", [P, 1])
        bq = sb(one, "bq", [3 * DC, 1])
        uq = sb(one, "uq", [QROWS, H * DK])
        qr = sb(one, "qr", [QROWS, H, DR])
        ukv = sb(one, "ukv", [2 * DC, H * DK])
        rows = sb(one, "rows", [96, P])
        wo = sb(one, "wo", [DK, H, D])
        bo = sb(one, "bo", [1, D])
        wm = sb(one, "wm", [P, KD, 6 * D])
        iota_i = sb(one, "iota_i", [P, 2 * E + 1], i32)
        silc = sb(one, "silc", [P, B, KD])
        silrep = sb(one, "silrep", [P, B, KD, P])
        bvrep = sb(one, "bvrep", [P, H, P])
        onesrow = sb(one, "onesrow", [1, P])
        shiftT = sb(one, "shiftT", [P, 4, B])
        uqT = sb(one, "uqT", [P, H, P])
        ukvT = sb(one, "ukvT", [P, H, 3 * DC])
        G = sb(one, "G", [QROWS, H, P])
        zeros = sb(one, "zeros", [P, 7 * D])
        stats = sb(one, "stats", [P, ST, 6])
        mv = sb(one, "mv", [P, ST, 2])
        vare = sb(one, "vare", [P, ST])
        rstd = sb(one, "rstd", [P, ST])
        xn = sb(one, "xn", [P, ST, D])
        hT = sb(one, "hT", [P, KD, S])

        t_ps = [ps(one, f"t_ps{n}", [P, HALF]) for n in range(3)]
        k_ps = ps(one, "k_ps", [P, S])
        q_ps = ps(one, "q_ps", [P, S])
        v_ps = ps(one, "v_ps", [P, ST, P], fp16)

        x_in = sem("x_in")
        const_p = sem("const_p")
        dve = sem("dve1")
        pe = sem("pe1")
        act = sem("act1")
        ln_var = sem("ln_var")
        ln_rstd = sem("ln_rstd")
        ln_xn = sem("ln_xn")
        xT_ready = sem("xT_ready")
        hT_ready = sem("hT_ready")
        kq_ready = sem("kq_ready")
        hi_done = sem("hi_done")
        lo_done = sem("lo_done")
        v_ready = sem("v_ready")
        v_done = sem("v_done")
        ln_v = sem("ln_v")
        ALL_LOADS = 16 * (2 + 4 + 8 + 12 + 4 + 3)

        with nc.Block() as block:
            @block.sync
            def _(sp):
                for b in range(B):
                    sp.dma_start(xs[:, b * ST:(b + 1) * ST, :],
                                 x_tiles[:, b * ST:(b + 1) * ST, :]).then_inc(x_in, 16)
                sp.dma_start(wm[:], wmod.rearrange("(k p) n -> p k n", p=P)).then_inc(loads, 16)
                sp.dma_start(wo[:], W_O.rearrange("(h d) n -> d h n", d=DK)).then_inc(loads, 16)
                sp.wait_ge(const_v, 1)
                for n in range((SLOTS + P) // (7 * P)):
                    sp.dma_start(xbuf[n * 7 * P:(n + 1) * 7 * P, :].rearrange("(p r) d -> p (r d)", p=P),
                                 zeros[:]).then_inc(zeroed, 16)
                sp.wait_ge(zeroed, 16 * ((SLOTS + P) // (7 * P)))

            @block.scalar
            def _(ac):
                def load(dst, src):
                    ac.dma_start(dst, src).then_inc(loads, 16)

                load(rows[0:64, :], b1.rearrange("e (f p) -> (e f) p", p=P))
                load(rows[64:80, :], router_w.rearrange("e (k p) -> (e k) p", p=P))
                load(rows[80:88, :], c.rearrange("b (k p) -> (b k) p", p=P))
                load(rows[88:96, :], b_UV.rearrange("(h d) -> h d", d=DK))
                for r in range(2):
                    load(wk[:, :, r * LR:r * LR + DC], W_DKV.rearrange("(k p) n -> p k n", p=P))
                    load(wk[:, :, r * LR + DC:(r + 1) * LR], W_KR.rearrange("(k p) n -> p k n", p=P))
                    load(bk[r * LR:r * LR + DC, :], b_DKV.rearrange("(p a) -> p a", a=1))
                    load(bk[r * LR + DC:(r + 1) * LR, :], b_KR.rearrange("(p a) -> p a", a=1))
                for r in range(3):
                    load(wq[:, :, r * DC:(r + 1) * DC], W_DQ.rearrange("(k p) n -> p k n", p=P))
                    load(bq[r * DC:(r + 1) * DC, :], b_DQ.rearrange("(p a) -> p a", a=1))
                    load(uq[r * DC:(r + 1) * DC, :], W_UQ)
                    load(qr[r * DC:(r + 1) * DC, :, :], W_QR.rearrange("c (h r) -> c h r", r=DR))
                for r in range(2):
                    row = b_UQ.rearrange("(a n) -> a n", a=1)
                    load(uq[3 * DC + r:3 * DC + r + 1, :], row)
                    load(qr[3 * DC + r:3 * DC + r + 1, :, :], b_QR.rearrange("(a h r) -> a h r", a=1, r=DR))
                load(ukv[0:DC, :], W_UK)
                load(ukv[DC:2 * DC, :], W_UV)
                load(bo[:], b_O.rearrange("(a n) -> a n", a=1))

                ac.wait_ge(dve, 1)
                nc.scalar.activation(silc[:], cols[:, 80:88].rearrange("p (b k) -> p b k", k=KD),
                                     ACT.Silu).then_inc(act, 1)
                for b in range(B):
                    for g in range(2):
                        for k in range(KD):
                            n = 4 * b + 2 * g + k
                            ac.wait_ge(const_v, 15)
                            ac.wait_ge(xT_ready, n + 1)
                            if n >= 1 and b >= 1 and g == 0 and k == 0:
                                ac.wait_ge(kq_ready, 2 * b)
                            nc.scalar.activation(hT[:, k, g * HALF:(g + 1) * HALF], t_ps[n % 2][:],
                                                 ACT.Identity, scale=shiftT[:, 2 + k, b:b + 1],
                                                 bias=shiftT[:, k, b:b + 1]).then_inc(hT_ready, 1)
                    ac.wait_ge(loads, ALL_LOADS)
                    ac.wait_ge(kq_ready, 2 * b + 1)
                    nc.scalar.activation(KA[:, b * S:(b + 1) * S], k_ps[:], ACT.Identity, bias=bk[:]).then_inc(hi_done, 1)
                    ac.wait_ge(kq_ready, 2 * b + 2)
                    nc.scalar.activation(CQ[0:3 * DC, b * S:(b + 1) * S], q_ps[0:3 * DC, :], ACT.Identity,
                                         bias=bq[:]).then_inc(hi_done, 1)

            @block.gpsimd
            def _(pool):
                nc.gpsimd.memset(ident[:], 0.0).then_inc(const_p, 1)
                nc.gpsimd.memset(ident16[:], 0.0).then_inc(const_p, 1)
                nc.gpsimd.memset(upto16[:], 1.0).then_inc(const_p, 1)
                pool.wait_ge(const_p, 3)
                for m in (ident, ident16):
                    nc.gpsimd.affine_select(out=m[:], in_=m[:], compare_op=ALU.not_equal, fill=1.0, base=0,
                                            pattern=[[-1, P]], channel_multiplier=1).then_inc(const_p, 1)
                nc.gpsimd.affine_select(out=upto16[:], in_=upto16[:], compare_op=ALU.is_ge, fill=0.0, base=0,
                                        pattern=[[1, P]], channel_multiplier=-1).then_inc(const_p, 1)
                nc.gpsimd.iota(iota_i[:, 0:E], pattern=[[-1, E]], base=E, channel_multiplier=0).then_inc(const_p, 1)
                nc.gpsimd.iota(iota_i[:, E:2 * E], pattern=[[CAP, E]], base=0, channel_multiplier=0).then_inc(const_p, 1)
                nc.gpsimd.iota(iota_i[:, 2 * E:2 * E + 1], pattern=[[0, 1]], base=SLOTS, channel_multiplier=1).then_inc(const_p, 1)
                fills = ((ones16[:], 1.0), (onesrow[:], 1.0), (mz[:], 0.0), (raw[:], 1.0), (VV[:, :, 2 * DC:P], 1.0),
                         (KB[LR:LR + 2, :], -1.0), (CQ[3 * DC:QROWS, :], 1.0))
                for n, (dst, value) in enumerate(fills):
                    pool.wait_ge(const_p, 9 + n)
                    nc.gpsimd.memset(dst, value).then_inc(const_p, 1)
                for b in range(B):
                    pool.wait_ge(const_p, 16)
                    pool.wait_ge(const_v, 2)
                    pool.wait_ge(ln_var, b + 1)
                    nc.gpsimd.tensor_tensor(rstd[:], vare[:], minus_half[:], ALU.pow).then_inc(ln_rstd, 1)

            @block.vector
            def _(v):
                nc.vector.memset(zeros[:], 0.0).then_inc(const_v, 1)
                nc.vector.memset(minus_half[:], -0.5).then_inc(const_v, 1)
                v.wait_ge(const_p, 9)
                nc.vector.tensor_copy(rev[:], iota_i[:, 0:E])
                nc.vector.tensor_copy(first_slot[:], iota_i[:, E:2 * E])
                nc.vector.tensor_copy(trash[:], iota_i[:, 2 * E:2 * E + 1])

                def norm(b):
                    v.wait_ge(x_in, 16 * (b + 1))
                    if b:
                        v.wait_ge(xT_ready, 4 * b)
                    for t in range(ST):
                        nc.vector.bn_stats(stats[:, t, :], xs[:, b * ST + t, :]).then_inc(ln_v, 1)
                    v.wait_ge(ln_v, b * (2 * ST) + ST)
                    for t in range(ST):
                        nc.vector.bn_aggr(mv[:, t, :], stats[:, t, :]).then_inc(ln_v, 1)
                    v.wait_ge(ln_v, (b + 1) * (2 * ST))
                    nc.vector.tensor_scalar(vare[:], mv[:, :, 1], EPS, None, ALU.add).then_inc(ln_var, 1)
                    v.wait_ge(ln_rstd, b + 1)
                    for t in range(ST):
                        nc.vector.tensor_scalar(xn[:, t, :], xs[:, b * ST + t, :], mv[:, t, 0:1],
                                                rstd[:, t:t + 1], ALU.subtract, ALU.mult).then_inc(ln_xn, 1)

                v.wait_ge(pe, 1)
                nc.vector.tensor_copy(cols[:], t_ps[0][:, 0:96]).then_inc(dve, 1)
                v.wait_ge(dve, 1)
                nc.vector.tensor_copy(bvrep[:], cols[:, 88:96].unsqueeze(2).broadcast_to([P, H, P])).then_inc(dve, 1)
                v.wait_ge(act, 1)
                nc.vector.tensor_copy(silrep[:], silc[:].unsqueeze(3).broadcast_to([P, B, KD, P])).then_inc(dve, 1)
                v.wait_ge(pe, 2)
                nc.vector.tensor_copy(shiftT[:, 0:2, :], t_ps[1][:, 0:2 * B].rearrange("p (m b) -> p m b", b=B)).then_inc(dve, 1)
                nc.vector.tensor_scalar(shiftT[:, 2:4, :], t_ps[1][:, 2 * B:4 * B].rearrange("p (m b) -> p m b", b=B),
                                        1.0, None, ALU.add).then_inc(dve, 1)
                for b in range(B):
                    v.wait_ge(pe, 3 + b)
                    nc.vector.tensor_copy(mod[:, b, :, :], (k_ps if b % 2 == 0 else q_ps)[:].rearrange("p (m d) -> p m d", m=4)).then_inc(const_v, 1)
                v.wait_ge(const_v, 6)
                scratch = hT[:, 0, :].rearrange("p (b d) -> p b d", b=B)
                v.wait_ge(dve, 5)
                for j in (GA, GB):
                    nc.vector.tensor_scalar(scratch, mod[:, :, j, :], 0.0, 2.0, ALU.is_ge, ALU.mult).then_inc(const_v, 1)
                    nc.vector.scalar_tensor_tensor(xn[:, 0:B, :], mod[:, :, j, :], -1.0, mod[:, :, j, :], ALU.mult, ALU.max).then_inc(const_v, 1)
                    v.wait_ge(const_v, 8 + (4 if j == GB else 0))
                    nc.vector.tensor_scalar(mod[:, :, j, :], xn[:, 0:B, :], 0.25, None, ALU.max).then_inc(const_v, 1)
                    v.wait_ge(const_v, 9 + (4 if j == GB else 0))
                    nc.vector.scalar_tensor_tensor(mod[:, :, j, :], scratch, -1.0, mod[:, :, j, :], ALU.add, ALU.mult).then_inc(const_v, 1)
                    v.wait_ge(const_v, 10 + (4 if j == GB else 0))
                nc.vector.tensor_scalar(mod[:, :, CB, :], mod[:, :, CB, :], 1.0, None, ALU.add).then_inc(const_v, 1)

                v.wait_ge(const_v, 15)
                norm(0)
                for g in range(2):
                    v.wait_ge(pe, 7 + g)
                    nc.vector.tensor_copy(uqT[:, 4 * g:4 * g + 4, 0:QROWS],
                                          t_ps[2][:, :].rearrange("p (h c) -> p h c", h=4)[:, :, 0:QROWS]).then_inc(dve, 1)
                v.wait_ge(pe, 9)
                kv = t_ps[2][:, :].rearrange("p (h c) -> p h c", h=H)
                nc.vector.tensor_copy(ukvT[:, :, 0:2 * DC], kv).then_inc(dve, 1)
                nc.vector.tensor_copy(ukvT[:, :, 2 * DC:3 * DC], kv[:, :, DC:2 * DC]).then_inc(dve, 1)
                v.wait_ge(pe, 10)
                g_ps = t_ps[2][0:QROWS, 0:H * DC].rearrange("p (h c) -> p h c", h=H)
                for r in range(2):
                    nc.vector.tensor_scalar(G[:, :, r * LR:r * LR + DC], g_ps, SCALE, None, ALU.mult).then_inc(dve, 1)
                    nc.vector.tensor_scalar(G[:, :, r * LR + DC:(r + 1) * LR], qr[:], SCALE, None, ALU.mult).then_inc(dve, 1)
                v.wait_ge(dve, 13)
                nc.vector.tensor_copy(GQ[:], G[:]).then_inc(dve, 1)
                v.wait_ge(dve, 14)
                nc.vector.tensor_tensor(GQ[64:QROWS, :, :], G[64:QROWS, :, :], GQ[64:QROWS, :, :], ALU.subtract).then_inc(dve, 1)
                v.wait_ge(dve, 15)
                nc.vector.tensor_copy(GQ[96:97, :, :], G[96:97, :, :]).then_inc(dve, 1)
                for g in range(2):
                    v.wait_ge(pe, 11 + g)
                    nc.vector.tensor_copy(proj[:, 2 * g:2 * g + 2, :], t_ps[2][:].rearrange("p (a d) -> p a d", a=2)).then_inc(dve, 1)
                v.wait_ge(pe, 13)
                nc.vector.tensor_copy(attn_bias[:], t_ps[2][:, 0:D]).then_inc(dve, 1)

                for b in range(B):
                    if b + 1 < B:
                        norm(b + 1)
                    v.wait_ge(hi_done, 2 * b + 2)
                    at = slice(b * S, (b + 1) * S)
                    nc.vector.scalar_tensor_tensor(KA[LR:P, at], k_ps[LR:P, :], bk[LR:P, :], KA[LR:P, at],
                                                   ALU.add, ALU.subtract).then_inc(lo_done, 1)
                    nc.vector.scalar_tensor_tensor(CQ[DC:2 * DC, at], q_ps[DC:2 * DC, :], bq[DC:2 * DC, :],
                                                   CQ[DC:2 * DC, at], ALU.add, ALU.subtract).then_inc(lo_done, 1)
                    nc.vector.tensor_copy(KB[0:LR, at], KA[0:LR, at])
                    v.wait_ge(v_ready, b + 1)
                    nc.vector.tensor_copy(VV[:, b * ST:(b + 1) * ST, 0:2 * DC].rearrange("p t (a c) -> p t a c", a=2),
                                          v_ps[:].rearrange("p t (a c) -> p t a c", c=DC)[:, :, 0:3:2, :]).then_inc(v_done, 1)

            @block.tensor
            def _(te):
                mm = nc.tensor.matmul
                te.wait_ge(const_p, 6)
                te.wait_ge(loads, ALL_LOADS)
                nc.tensor.transpose(t_ps[0][:, 0:96], rows[:], ident[0:96, 0:96]).then_inc(pe, 1)
                te.wait_ge(act, 1)
                for m in range(4):
                    for k in range(KD):
                        last = mm(t_ps[1][:, m * B:(m + 1) * B], wm[:, k, m * P:(m + 1) * P], silc[:, :, k],
                                  start=k == 0, stop=k == KD - 1)
                last.then_inc(pe, 1)
                te.wait_ge(dve, 3)
                for b in range(B):
                    o = k_ps if b % 2 == 0 else q_ps
                    if b >= 2:
                        te.wait_ge(const_v, b + 1)
                    for n in range(2):
                        for k in range(KD):
                            last = mm(o[:, n * HALF:(n + 1) * HALF], silrep[:, b, k, :],
                                      wm[:, k, 2 * D + n * HALF:2 * D + (n + 1) * HALF], start=k == 0, stop=k == KD - 1)
                    last.then_inc(pe, 1)
                for g in range(2):
                    if g:
                        te.wait_ge(dve, 6)
                    for h in range(4):
                        last = nc.tensor.transpose(t_ps[2][:, h * P:h * P + QROWS], uq[:, (4 * g + h) * DK:(4 * g + h + 1) * DK],
                                                   ident[0:QROWS, 0:QROWS])
                    last.then_inc(pe, 1)
                te.wait_ge(dve, 7)
                for h in range(H):
                    last = nc.tensor.transpose(t_ps[2][:, h * 2 * DC:(h + 1) * 2 * DC], ukv[:, h * DK:(h + 1) * DK],
                                               ident[0:2 * DC, 0:2 * DC])
                last.then_inc(pe, 1)
                te.wait_ge(dve, 9)
                for h in range(H):
                    last = mm(t_ps[2][0:QROWS, h * DC:(h + 1) * DC], uqT[:, h, 0:QROWS], ukvT[:, h, 0:DC], start=True, stop=True)
                last.then_inc(pe, 1)
                te.wait_ge(dve, 13)
                for g in range(2):
                    if g:
                        te.wait_ge(dve, 17)
                    for h in range(4 * g, 4 * g + 4):
                        r = 2 * DC * (h % 2)
                        a = (h // 2) % 2
                        last = mm(t_ps[2][r:r + 2 * DC, a * D:(a + 1) * D], ukvT[:, h, DC:3 * DC], wo[:, h, :], start=True, stop=True)
                    last.then_inc(pe, 1)
                te.wait_ge(dve, 18)
                for h in range(H):
                    mm(t_ps[2][:, 0:D], bvrep[:, h, :], wo[:, h, :], start=h == 0, stop=False)
                mm(t_ps[2][:, 0:D], onesrow[:], bo[:], start=False, stop=True).then_inc(pe, 1)

                for b in range(B):
                    for g in range(2):
                        te.wait_ge(ln_xn, b * ST + 4 * g + 4)
                        for k in range(KD):
                            n = 4 * b + 2 * g + k
                            if n >= 2:
                                te.wait_ge(hT_ready, n - 1)
                            for t in range(4):
                                last = nc.tensor.transpose(t_ps[n % 2][:, t * P:(t + 1) * P],
                                                           xn[:, 4 * g + t, k * P:(k + 1) * P], ident[:])
                            last.then_inc(xT_ready, 1)
                    te.wait_ge(hT_ready, 4 * b + 4)
                    if b == 0:
                        te.wait_ge(const_v, 6)
                    else:
                        te.wait_ge(lo_done, 2 * b)
                    for o, w, m in ((k_ps, wk, P), (q_ps, wq, 3 * DC)):
                        for g in range(2):
                            for k in range(KD):
                                last = mm(o[0:m, g * HALF:(g + 1) * HALF], w[:, k, :], hT[:, k, g * HALF:(g + 1) * HALF],
                                          start=k == 0, stop=k == KD - 1)
                        last.then_inc(kq_ready, 1)
                    te.wait_ge(lo_done, 2 * b + 2)
                    if b:
                        te.wait_ge(v_done, b)
                    for t in range(ST):
                        last = nc.tensor.transpose(v_ps[:, t, :], KA[:, b * S + t * P:b * S + (t + 1) * P], ident16[:])
                    last.then_inc(v_ready, 1)
        one.close()

        two = inner
        latents = ExitStack()
        o_n = latents.enter_context(nc.sbuf_tensor("o_n", [P, H // 2, N], fp32, side="right"))
        QA = sb(two, "QA", [P, 4, S], fp16)
        QB = sb(two, "QB", [LR + 2, 4, S], fp16)
        prob = sb(two, "prob", [P, 4, S])
        prob_hi = sb(two, "prob_hi", [P, 4, S], fp16)
        prob_lo = sb(two, "prob_lo", [P, 2, S], fp16)
        part_max = sb(two, "part_max", [P, ST, 2])
        row_max = sb(two, "row_max", [P, ST])
        st_ps = [ps(two, f"st_ps{n}", [P, S]) for n in range(2)]
        acc_ps = ps(two, "acc_ps", [P, S])
        x_ps = [ps(two, f"x_ps{n}", [P, HALF]) for n in range(2)]

        scores_ready = sem("scores_ready")
        exp_done = sem("exp_done")
        cast_a = sem("cast_a")
        cast_p = sem("cast_p")
        sub_d = sem("sub_d")
        sub_p = sem("sub_p")
        pv_done = sem("pv_done")
        smax_ready = sem("smax_ready")
        smax_done = sem("smax_done")
        q_ready = sem("q_ready")
        qa_done = sem("qa_done")
        ql_done = sem("ql_done")
        split_done = sem("split_done")
        mrow_ready = sem("mrow_ready")
        mrow_done = sem("mrow_done")
        raw_done = sem("raw_done")
        rinv_done = sem("rinv_done")
        norm_done = sem("norm_done")
        HALVES = (0, 1)
        SIXTEEN = tuple(range(16))
        STEPS = (0, 1, 2)
        ONCE = (0,)

        def cast_of(k):
            return (cast_a, CAST_ACT) if k in CAST_ACT else (cast_p, CAST_POOL)

        def sub_of(k):
            return (sub_d, SUB_DVE) if k in SUB_DVE else (sub_p, SUB_POOL)

        def after(t, u, pair, k):
            events = pair[1]
            return 4 * len(events) * t + ((u + 1) * len(events) + events.index(k) + 1)

        def place(t, u):
            if u >= 4:
                t, u = (t + 1) & 7, u - 4
            if u < 0:
                t, u = (t + 7) & 7, u + 4
            b = t >> 1
            return (b if isinstance(t, int) else b.with_bounds(min_val=0, max_val=B - 1)), (t & 1) * 4 + u

        def ahead(u, k, n):
            return u + (k + n) // 8, (k + n) % 8

        def slots(body, t, head_range, k_range=ALL):
            for u in head_range:
                for k in k_range:
                    body(t, u, k)

        with nc.Block() as block:
            @block.tensor
            def _(te):
                mm = nc.tensor.matmul

                def queries(t, j):
                    b, h = place(t, j)
                    for f in HALVES:
                        te.wait_ge(smax_done, after(t, j - 1, (0, SIXTEEN), 14 + f))
                        mm(x_ps[f][:], GQ[:, bass.ds(h, 1), :].rearrange("p a c -> p (a c)"),
                           CQ[:, bass.ds(b * S + f * HALF, HALF)], start=True, stop=True).then_inc(q_ready, 1)

                def max_scores(t, j, q):
                    b, _ = place(t, j)
                    if q == 0:
                        te.wait_ge(qa_done, after(t, j, (0, HALVES), 1))
                    for f in HALVES:
                        if q == 0:
                            te.wait_ge(mrow_done, after(t, j - 1, (0, HALVES), f))
                            te.wait_ge(ql_done, after(t, j, (0, HALVES), f))
                        else:
                            te.wait_ge(smax_done, after(t, j, (0, SIXTEEN), 2 * (q - 1) + f))
                        mm(x_ps[f][:], QA[:, j % 4, q * P:(q + 1) * P], KA[:, bass.ds(b * S + f * HALF, HALF)],
                           start=True, stop=True).then_inc(smax_ready, 1)

                def max_rows(t, j):
                    te.wait_ge(split_done, after(t, j, (0, STEPS), 2))
                    for f in HALVES:
                        te.wait_ge(qa_done, after(t, j + 1, (0, HALVES), f))
                        te.wait_ge(ql_done, after(t, j + 1, (0, HALVES), f))
                        for q in range(4):
                            last = mm(x_ps[f][0:LR + 2, q * P:(q + 1) * P], mz[:, 4 * f + q, :], ident16[:],
                                      start=True, stop=True)
                        last.then_inc(mrow_ready, 1)

                def scores(t, j, k):
                    b, _ = place(t, j)
                    pj, pk = ahead(j, k, -2)
                    if k == 0:
                        te.wait_ge(ql_done, after(t, j, (0, HALVES), 1))
                        te.wait_ge(mrow_done, after(t, j, (0, HALVES), 1))
                    te.wait_ge(exp_done, after(t, pj, (0, ALL), pk))
                    for keys, q, r, first in ((KA, QA, P, True), (KB, QB, LR + 2, False)):
                        for f in HALVES:
                            last = mm(st_ps[k % 2][:, f * HALF:(f + 1) * HALF], keys[0:r, bass.ds(b * S + k * P, P)],
                                      q[0:r, j % 4, f * HALF:(f + 1) * HALF], start=first, stop=not first)
                    last.then_inc(scores_ready, 1)

                def values(t, u, k):
                    b, _ = place(t, u)
                    if k == 0:
                        te.wait_ge(raw_done, after(t, u - 1, (0, ONCE), 0))
                    te.wait_ge(cast_of(k)[0], after(t, u, cast_of(k), k))
                    te.wait_ge(sub_of(k)[0], after(t, u, sub_of(k), k))
                    for part, slots_of in ((prob_hi, 4), (prob_lo, 2)):
                        for f in HALVES:
                            last = mm(acc_ps[:, f * HALF:(f + 1) * HALF],
                                      VV[:, bass.ds(b * ST + k, 1), :].rearrange("p a c -> p (a c)"),
                                      part[:, k % slots_of, f * HALF:(f + 1) * HALF],
                                      start=k == 0 and part is prob_hi, stop=k == 7 and part is prob_lo)
                    last.then_inc(pv_done, 1)

                def look_ahead(t, u, k):
                    if k < 4:
                        max_scores(t, u + 1, k + 4)
                    if k == 4:
                        queries(t, u + 2)
                        max_rows(t, u + 1)
                    if k >= 4:
                        max_scores(t, u + 2, k - 4)

                def slot(t, u, k):
                    scores(t, *ahead(u, k, 2))
                    look_ahead(t, u, k)
                    values(t, u, k)

                for sm, n in ((scores_ready, 8), (pv_done, 8), (smax_ready, 16), (q_ready, 2), (mrow_ready, 2)):
                    te.sem_inc(sm, n)
                queries(0, 0)
                for q in range(4):
                    max_scores(0, 0, q)
                for k in ALL:
                    if k >= 6:
                        scores(0, *ahead(-1, k, 2))
                    look_ahead(0, -1, k)
                with te.Fori(0, B * H // 4) as t:
                    slots(slot, t, range(4))

            @block.scalar
            def _(ac):
                def exponentials(t, j, k):
                    ac.wait_ge(scores_ready, after(t, j, (0, ALL), k))
                    pj, pk = ahead(j, k, -4)
                    ac.wait_ge(sub_of(pk)[0], after(t, pj, sub_of(pk), pk))
                    nc.scalar.activation(prob[:, k % 4, :], st_ps[k % 2][:], ACT.Exp).then_inc(exp_done, 1)

                def query_high(t, j):
                    for f in HALVES:
                        ac.wait_ge(q_ready, after(t, j, (0, HALVES), f))
                        nc.scalar.activation(QA[:, j % 4, f * HALF:(f + 1) * HALF], x_ps[f][:], ACT.Copy).then_inc(qa_done, 1)

                def max_rows_out(t, j):
                    for f in HALVES:
                        ac.wait_ge(mrow_ready, after(t, j, (0, HALVES), f))
                        nc.scalar.activation(QB[LR:LR + 2, j % 4, f * HALF:(f + 1) * HALF], x_ps[f][LR:LR + 2, :],
                                             ACT.Copy).then_inc(mrow_done, 1)

                def round_probs(t, j, k):
                    pj, pk = ahead(j, k, -4)
                    ac.wait_ge(exp_done, after(t, j, (0, ALL), k))
                    ac.wait_ge(pv_done, after(t, pj, (0, ALL), pk))
                    nc.scalar.activation(prob_hi[:, k % 4, :], prob[:, k % 4, :], ACT.Copy).then_inc(cast_a, 1)

                def ahead_part(t, u, k):
                    if k == 4:
                        query_high(t, u + 2)
                        max_rows_out(t, u + 1)
                    if k >= 6 or u >= 0:
                        exponentials(t, *ahead(u, k, 2))
                    j, kk = ahead(u, k, 1)
                    if (k == 7 or u >= 0) and kk in CAST_ACT:
                        round_probs(t, j, kk)

                def slot(t, u, k):
                    ahead_part(t, u, k)
                    if k == 0:
                        ac.wait_ge(raw_done, after(t, u - 1, (0, ONCE), 0))
                        ac.wait_ge(norm_done, after(t, u - 1, (0, ONCE), 0))
                        nc.scalar.activation(rinv[:], raw[LR:P, :], ACT.Ln).then_inc(rinv_done, 1)
                        ac.wait_ge(rinv_done, after(t, u - 1, (0, HALVES), 0))
                        nc.scalar.activation(rinv[:], rinv[:], ACT.Exp, scale=-1.0).then_inc(rinv_done, 1)
                    if k == 7:
                        ac.wait_ge(pv_done, after(t, u, (0, ALL), 7))
                        ac.wait_ge(norm_done, after(t, u, (0, ONCE), 0))
                        nc.scalar.activation(raw[:], acc_ps[:], ACT.Copy).then_inc(raw_done, 1)

                for sm, n in ((exp_done, 8), (cast_a, len(CAST_ACT)), (qa_done, 2), (mrow_done, 2), (raw_done, 1)):
                    ac.sem_inc(sm, n)
                query_high(0, 0)
                slots(ahead_part, 0, (-1,))
                with ac.Fori(0, B * H // 4) as t:
                    slots(slot, t, range(4))
                ac.wait_ge(raw_done, B * H + 1)
                nc.scalar.activation(rinv[:], raw[LR:P, :], ACT.Ln).then_inc(rinv_done, 1)
                ac.wait_ge(rinv_done, 2 * B * H + 1)
                nc.scalar.activation(rinv[:], rinv[:], ACT.Exp, scale=-1.0).then_inc(rinv_done, 1)

            @block.gpsimd
            def _(pool):
                def part(t, j, k):
                    pj, pk = ahead(j, k, -4)
                    if k in CAST_POOL:
                        wait_apart(pool, (exp_done, after(t, j, (0, ALL), k)), (pv_done, after(t, pj, (0, ALL), pk)))
                        nc.gpsimd.tensor_scalar(prob_hi[:, k % 4, :], prob[:, k % 4, :], 1.0, 1.0,
                                                ALU.mult, ALU.mult).then_inc(cast_p, 1)
                    if k in SUB_POOL:
                        pj, pk = ahead(j, k, -2)
                        pool.wait_ge(pv_done, after(t, pj, (0, ALL), pk))
                        pool.wait_ge(cast_of(k)[0], after(t, j, cast_of(k), k))
                        nc.gpsimd.tensor_tensor(prob_lo[:, k % 2, :], prob[:, k % 4, :], prob_hi[:, k % 4, :],
                                                ALU.subtract).then_inc(sub_p, 1)

                pool.sem_inc(cast_p, len(CAST_POOL))
                pool.sem_inc(sub_p, len(SUB_POOL))
                part(0, 0, 0)
                with pool.Fori(0, B * H // 4) as t:
                    slots(lambda t, u, k: part(t, *ahead(u, k, 1)), t, range(4))

            @block.vector
            def _(v):
                def query_low(t, j):
                    for f in HALVES:
                        v.wait_ge(qa_done, after(t, j, (0, HALVES), f))
                        at = slice(f * HALF, (f + 1) * HALF)
                        nc.vector.tensor_tensor(QB[0:LR, j % 4, at], x_ps[f][0:LR, :], QA[0:LR, j % 4, at],
                                                ALU.subtract).then_inc(ql_done, 1)

                def maxima(t, j, q):
                    for f in HALVES:
                        v.wait_ge(smax_ready, after(t, j, (0, SIXTEEN), 2 * q + f))
                        nc.vector.tensor_reduce(part_max[:, q, f:f + 1], x_ps[f][:], AX.X, ALU.max).then_inc(smax_done, 1)

                def split_maxima(t, j):
                    v.wait_ge(smax_done, after(t, j, (0, SIXTEEN), 15))
                    nc.vector.tensor_tensor(row_max[:], part_max[:, :, 0], part_max[:, :, 1], ALU.max).then_inc(split_done, 1)
                    v.wait_ge(mrow_ready, after(t, j - 1, (0, HALVES), 1))
                    v.wait_ge(split_done, after(t, j, (0, STEPS), 0))
                    nc.vector.tensor_copy(mz[:, :, LR], row_max[:]).then_inc(split_done, 1)
                    v.wait_ge(split_done, after(t, j, (0, STEPS), 1))
                    nc.vector.tensor_tensor(mz[:, :, LR + 1], row_max[:], mz[:, :, LR], ALU.subtract).then_inc(split_done, 1)

                def low_probs(t, j, k):
                    pj, pk = ahead(j, k, -2)
                    v.wait_ge(pv_done, after(t, pj, (0, ALL), pk))
                    v.wait_ge(cast_of(k)[0], after(t, j, cast_of(k), k))
                    nc.vector.tensor_tensor(prob_lo[:, k % 2, :], prob[:, k % 4, :], prob_hi[:, k % 4, :],
                                            ALU.subtract).then_inc(sub_d, 1)

                def normalise(t, u):
                    b, h = place(t, u)
                    r = LR * (u % 2)
                    v.wait_ge(rinv_done, after(t, u, (0, HALVES), 1))
                    nc.vector.tensor_tensor(o_n[r:r + LR, bass.ds(h >> 1, 1), bass.ds(b * S, S)].rearrange("p a n -> p (a n)"),
                                            raw[0:LR, :], rinv[:], ALU.mult).then_inc(norm_done, 1)

                def ahead_part(t, u, k):
                    if k < 4:
                        maxima(t, u + 1, k + 4)
                    if k == 3:
                        split_maxima(t, u + 1)
                    if k == 4:
                        query_low(t, u + 2)
                    if k >= 4:
                        maxima(t, u + 2, k - 4)
                    j, kk = ahead(u, k, 1)
                    if (k == 7 or u >= 0) and kk in SUB_DVE:
                        low_probs(t, j, kk)

                def slot(t, u, k):
                    ahead_part(t, u, k)
                    if k == 1:
                        normalise(t, u - 1)

                for sm, n in ((smax_done, 16), (ql_done, 2), (split_done, 3), (sub_d, len(SUB_DVE)), (norm_done, 1)):
                    v.sem_inc(sm, n)
                query_low(0, 0)
                for q in range(4):
                    maxima(0, 0, q)
                slots(ahead_part, 0, (-1,))
                with v.Fori(0, B * H // 4) as t:
                    slots(slot, t, range(4))
                v.wait_ge(rinv_done, 2 * B * H + 2)
                nc.vector.tensor_tensor(o_n[LR:P, H // 2 - 1, (B - 1) * S:N], raw[0:LR, :], rinv[:],
                                        ALU.mult).then_inc(norm_done, 1)
        inner.close()

        three = ExitStack()
        stage = sb(three, "stage", [P, 2, H // 2, P])
        projb = sb(three, "projb", [P, H // 2, D])
        gbias = sb(three, "gbias", [P, D])
        hs = sb(three, "hs", [P, 2, ST, D])
        hsT = sb(three, "hsT", [P, 2, KD, P])
        st3 = sb(three, "st3", [P, ST, 6])
        mv3 = sb(three, "mv3", [P, ST, 2])
        var3 = sb(three, "var3", [P, ST])
        rstd3 = sb(three, "rstd3", [P, ST])
        top = sb(three, "top", [P, ST])
        below = sb(three, "below", [P, ST, E])
        ex = sb(three, "ex", [P, ST, E])
        ranked = sb(three, "ranked", [P, ST, E])
        best = sb(three, "best", [P, ST])
        onehot = sb(three, "onehot", [P, ST, E], fp16)
        cum = sb(three, "cum", [P, ST + 1, E], fp16)
        picked = sb(three, "picked", [P, ST, E])
        pos = sb(three, "pos", [P, ST])
        start_of = sb(three, "start_of", [P, ST])
        kept = sb(three, "kept", [P, ST])
        slot_f = sb(three, "slot_f", [P, ST])
        moved = sb(three, "moved", [P, ST])
        total = sb(three, "total", [P, ST])
        recip = sb(three, "recip", [P, ST])
        to_slot = sb(three, "to_slot", [P, 2, ST], u32)
        a_ps = [ps(three, f"a_ps{n}", [P, HALF]) for n in range(2)]
        tr_ps = [ps(three, f"tr_ps{n}", [P, KD, P]) for n in range(2)]
        lg_ps = ps(three, "lg_ps", [P, ST, E])
        pos_ps = ps(three, "pos_ps", [P, ST, E])

        biased = sem("biased")
        gbias_done = sem("gbias_done")
        scaled = sem("scaled")
        staged = sem("staged")
        projected = sem("projected")
        x1_done = sem("x1_done")
        stat3 = sem("stat3")
        var3_done = sem("var3_done")
        rstd3_done = sem("rstd3_done")
        centred = sem("centred")
        modulated = sem("modulated")
        turned = sem("turned")
        turned_out = sem("turned_out")
        logits = sem("logits")
        exps3 = sem("exps3")
        route = sem("route")
        pos_ready = sem("pos_ready")
        scattered = [sem(f"scattered{n}") for n in range(2)]
        rows_free = sem("rows_free")
        NROUTE = 27
        KR = tuple(range(NROUTE))

        def upto(t, u, n, k):
            return 2 * n * t + ((u + 1) * n + k + 1)

        with nc.Block() as block:
            @block.sync
            def _(sp):
                sp.sem_inc(rows_free, 2)
                with sp.Fori(0, B // 2) as t:
                    for u in range(2):
                        sp.wait_ge(scattered[u], 16 * ST * (t + 1))
                        sp.sem_inc(rows_free, 1)

            @block.scalar
            def _(ac):
                for sm, n in ((staged, ST), (turned_out, ST), (exps3, 1)):
                    ac.sem_inc(sm, n)
                with ac.Fori(0, B // 2) as t:
                    for u in range(2):
                        for n in range(2 * ST):
                            if n < ST:
                                ac.wait_ge(projected, upto(t, u, ST, n - 2))
                                nc.scalar.activation(stage[:, n % 2, :, :], o_n[:, :, bass.ds((2 * t + u) * S + n * P, P)],
                                                     ACT.Copy).then_inc(staged, 1)
                            else:
                                m = n - ST
                                ac.wait_ge(turned, upto(t, u, ST, m))
                                nc.scalar.activation(hsT[:, m % 2, :, :], tr_ps[m % 2][:], ACT.Copy).then_inc(turned_out, 1)
                        ac.wait_ge(route, upto(t, u, NROUTE, 1))
                        nc.scalar.activation(ex[:], below[:], ACT.Exp).then_inc(exps3, 1)

            @block.gpsimd
            def _(pool):
                for b in range(B):
                    if b:
                        pool.wait_ge(biased, b)
                    nc.gpsimd.tensor_tensor(gbias[:], attn_bias[:], mod[:, b, GA, :], ALU.mult).then_inc(gbias_done, 1)
                    pool.wait_ge(gbias_done, b + 1)
                    nc.gpsimd.tensor_tensor(x1[:, b * ST:(b + 1) * ST, :], x1[:, b * ST:(b + 1) * ST, :],
                                            gbias[:].unsqueeze(1).broadcast_to([P, ST, D]), ALU.add).then_inc(biased, 1)
                for sm, n in ((rstd3_done, 2), (modulated, 2 * ST)):
                    pool.sem_inc(sm, n)
                with pool.Fori(0, B // 2) as t:
                    for u in range(2):
                        for g in range(2):
                            pool.wait_ge(var3_done, upto(t, u, 2, g))
                            nc.gpsimd.tensor_tensor(rstd3[:, 4 * g:4 * g + 4], var3[:, 4 * g:4 * g + 4],
                                                    minus_half[:, 0:4], ALU.pow).then_inc(rstd3_done, 1)
                            for n in range(4 * g, 4 * g + 4):
                                wait_apart(pool, (centred, upto(t, u, ST, n)))
                                nc.gpsimd.tensor_tensor(hs[:, u, n, :], hs[:, u, n, :],
                                                        mod[:, bass.ds(2 * t + u, 1), CB, :].rearrange("p a d -> p (a d)"),
                                                        ALU.mult).then_inc(modulated, 1)
                                wait_apart(pool, (modulated, upto(t, u, 2 * ST, 2 * n)))
                                nc.gpsimd.tensor_tensor(hs[:, u, n, :], hs[:, u, n, :],
                                                        mod[:, bass.ds(2 * t + u, 1), SB_, :].rearrange("p a d -> p (a d)"),
                                                        ALU.add).then_inc(modulated, 1)
                        pool.wait_ge(zeroed, 16 * ((SLOTS + P) // (7 * P)))
                        pool.wait_ge(route, upto(t, u, NROUTE, NROUTE - 1))
                        wait_apart(pool, (modulated, upto(t, u, 2 * ST, 2 * ST - 1)))
                        for n in range(ST):
                            nc.gpsimd.indirect_dma_start(
                                out=xbuf, out_offset=bass.IndirectOffsetOnAxis(ap=to_slot[:, u, n:n + 1], axis=0),
                                in_=hs[:, u, n, :], in_offset=None).then_inc(scattered[u], 16)
                for u in range(2):
                    pool.wait_ge(scattered[u], 16 * ST * B // 2)

            @block.vector
            def _(v):
                def centre(v, t, u, g):
                    v.wait_ge(rstd3_done, upto(t, u, 2, g))
                    for n in range(4 * g, 4 * g + 4):
                        nc.vector.tensor_scalar(hs[:, u, n, :],
                                                x1[:, bass.ds((2 * t + u) * ST + n, 1), :].rearrange("p a d -> p (a d)"),
                                                mv3[:, n, 0:1], rstd3[:, n:n + 1], ALU.subtract, ALU.mult).then_inc(centred, 1)

                def routing(v, t, u):
                    made = [0]

                    def step(ins, wait=True):
                        ins.then_inc(route, 1)
                        v.wait_ge(route, upto(t, u, NROUTE, made[0]))
                        made[0] += 1

                    def wide(ap):
                        return ap.unsqueeze(2).broadcast_to([P, ST, E])

                    rev_w = rev[:].unsqueeze(1).broadcast_to([P, ST, E])
                    first_w = first_slot[:].unsqueeze(1).broadcast_to([P, ST, E])
                    at = bass.ds((2 * t + u) * ST, ST)
                    V = nc.vector
                    v.wait_ge(logits, upto(t, u, ST, ST - 1))
                    step(V.tensor_reduce(top[:], lg_ps[:], AX.X, ALU.max))
                    v.wait_ge(exps3, upto(t, u, 1, -1))
                    step(V.tensor_tensor(below[:], lg_ps[:], wide(top[:]), ALU.subtract))
                    step(V.scalar_tensor_tensor(ranked[:], below[:], 0.0, rev_w, ALU.is_equal, ALU.mult))
                    step(V.tensor_reduce(best[:], ranked[:], AX.X, ALU.max))
                    v.wait_ge(pos_ready, upto(t, u, 1, -1))
                    step(V.tensor_tensor(onehot[:], rev_w, wide(best[:]), ALU.is_equal))
                    step(V.tensor_copy(cum[:, 0, :], cum[:, ST, :]))
                    for n in range(ST):
                        step(V.tensor_tensor(cum[:, n + 1, :], cum[:, n, :], onehot[:, n, :], ALU.add))
                    v.wait_ge(pos_ready, upto(t, u, 1, 0))
                    step(V.tensor_tensor(picked[:], pos_ps[:], onehot[:], ALU.mult))
                    step(V.tensor_reduce(pos[:], picked[:], AX.X, ALU.add))
                    step(V.tensor_tensor(ranked[:], first_w, onehot[:], ALU.mult))
                    step(V.tensor_reduce(start_of[:], ranked[:], AX.X, ALU.add))
                    step(V.tensor_scalar(kept[:], pos[:], float(CAP), None, ALU.is_le))
                    step(V.tensor_scalar(moved[:], pos[:], float(CAP), -1.0, ALU.min, ALU.add))
                    step(V.tensor_tensor(slot_f[:], moved[:], start_of[:], ALU.add))
                    step(V.tensor_copy(slot_of[:, at], slot_f[:]))
                    step(V.scalar_tensor_tensor(moved[:], slot_f[:], trash[:], kept[:], ALU.subtract, ALU.mult))
                    v.wait_ge(rows_free, 2 * t + (u + 1))
                    step(V.tensor_scalar(to_slot[:, u, :], moved[:], trash[:], None, ALU.add))
                    v.wait_ge(exps3, upto(t, u, 1, 0))
                    step(V.tensor_reduce(total[:], ex[:], AX.X, ALU.add))
                    step(V.reciprocal(recip[:], total[:]))
                    step(V.tensor_tensor(gate_of[:, at], recip[:], kept[:], ALU.mult))
                    assert made[0] == NROUTE

                nc.vector.memset(cum[:, ST, :], 0.0).then_inc(dve, 1)
                v.wait_ge(dve, 20)
                for sm, n in ((x1_done, ST), (stat3, 2 * ST), (var3_done, 2), (centred, ST), (route, NROUTE)):
                    v.sem_inc(sm, n)
                with v.Fori(0, B // 2) as t:
                    for u in range(2):
                        b = 2 * t + u
                        v.wait_ge(projected, upto(t, u, ST, -1))
                        nc.vector.tensor_tensor(projb[:], proj[:],
                                                mod[:, bass.ds(b, 1), GA, :].broadcast_to([P, H // 2, D]), ALU.mult).then_inc(scaled, 1)
                        v.wait_ge(rows_free, 2 * t + (u + 1))
                        v.wait_ge(biased, b + 1)
                        for g in range(2):
                            for n in range(4 * g, 4 * g + 4):
                                v.wait_ge(projected, upto(t, u, ST, n))
                                row = x1[:, bass.ds(b * ST + n, 1), :].rearrange("p a d -> p (a d)")
                                nc.vector.tensor_tensor(row, a_ps[n % 2][:, 0:D], row, ALU.add).then_inc(x1_done, 1)
                                wait_apart(v, (x1_done, upto(t, u, ST, n)))
                                nc.vector.bn_stats(st3[:, n, :], row).then_inc(stat3, 1)
                                wait_apart(v, (stat3, upto(t, u, 2 * ST, 2 * n)))
                                nc.vector.bn_aggr(mv3[:, n, :], st3[:, n, :]).then_inc(stat3, 1)
                            v.wait_ge(stat3, upto(t, u, 2 * ST, 8 * g + 7))
                            nc.vector.tensor_scalar(var3[:, 4 * g:4 * g + 4], mv3[:, 4 * g:4 * g + 4, 1], EPS, None,
                                                    ALU.add).then_inc(var3_done, 1)
                            if g == 1:
                                centre(v, t, u, 0)
                        centre(v, t, u, 1)
                        routing(v, t, u)

            @block.tensor
            def _(te):
                mm = nc.tensor.matmul

                def project(t, u, n):
                    te.wait_ge(staged, upto(t, u, ST, n))
                    if n == 0:
                        te.wait_ge(scaled, 2 * t + u + 1)
                    te.wait_ge(x1_done, upto(t, u, ST, n - 2))
                    for a in range(H // 2):
                        last = mm(a_ps[n % 2][:, 0:D], stage[:, n % 2, a, :], projb[:, a, :], start=a == 0, stop=a == H // 2 - 1)
                    last.then_inc(projected, 1)

                def turn(t, u, n):
                    te.wait_ge(modulated, upto(t, u, 2 * ST, 2 * n + 1))
                    te.wait_ge(turned_out, upto(t, u, ST, n - 2))
                    for k in range(KD):
                        last = nc.tensor.transpose(tr_ps[n % 2][:, k, :], hs[:, u, n, k * P:(k + 1) * P], ident[:])
                    last.then_inc(turned, 1)

                def route_logits(t, u, n):
                    te.wait_ge(turned_out, upto(t, u, ST, n))
                    if n == 0:
                        te.wait_ge(route, upto(t, u, NROUTE, 1 - NROUTE))
                    for k in range(KD):
                        last = mm(lg_ps[:, n, :], hsT[:, n % 2, k, :], rwT[:, k, :], start=k == 0, stop=k == KD - 1)
                    last.then_inc(logits, 1)

                for sm, n in ((projected, ST), (turned, ST), (logits, ST), (pos_ready, 1)):
                    te.sem_inc(sm, n)
                with te.Fori(0, B // 2) as t:
                    for u in range(2):
                        for n in range(ST):
                            project(t, u, n)
                        for n in range(ST):
                            turn(t, u, n)
                            if n:
                                route_logits(t, u, n - 1)
                        route_logits(t, u, ST - 1)
                        te.wait_ge(route, upto(t, u, NROUTE, 4 + 1 + ST))
                        flat = pos_ps[:].rearrange("p t e -> p (t e)")
                        mm(flat, upto16[:], onehot[:].rearrange("p t e -> p (t e)"), start=True, stop=False)
                        mm(flat, ones16[:], cum[:, 0:ST, :].rearrange("p t e -> p (t e)"), start=False, stop=True).then_inc(pos_ready, 1)
        three.close()
        latents.close()

        four = ExitStack()
        w1f = sb(four, "w1f", [P, 2, KD, F])
        w2f = sb(four, "w2f", [P, 2, FT, D])
        w1h = sb(four, "w1h", [P, 2, KD, F], fp16)
        w1l = sb(four, "w1l", [P, 2, KD, F], fp16)
        w2h = sb(four, "w2h", [P, 2, FT, D], fp16)
        w2l = sb(four, "w2l", [P, 2, FT, D], fp16)
        b2w = sb(four, "b2w", [P, 2, D])
        b1c = sb(four, "b1c", [P, 2, FT])
        xb = sb(four, "xb", [P, 2, ET, D])
        xh = sb(four, "xh", [P, 2, KD * CAP], fp16)
        xl = sb(four, "xl", [P, 2, KD * CAP], fp16)
        act_f = sb(four, "act_f", [P, 2, CAP])
        act_h = sb(four, "act_h", [P, FT, CAP], fp16)
        act_l = sb(four, "act_l", [P, FT, CAP], fp16)
        yo = sb(four, "yo", [P, 2, ET, D])
        NW = CAP // 2
        xt_ps = [ps(four, f"xt_ps{n}", [P, HALF]) for n in range(2)]
        g_ps4 = [ps(four, f"g_ps{n}", [P, 2, HALF]) for n in range(2)]
        y_ps = [ps(four, f"y_ps{n}", [P, HALF]) for n in range(2)]

        w_in = [sem(f"w_in{n}") for n in range(2)]
        b2_in = [sem(f"b2_in{n}") for n in range(2)]
        split_w = sem("split_w")
        split_v = sem("split_v")
        xt_ready = sem("xt_ready")
        xh_done = sem("xh_done")
        xl_done = sem("xl_done")
        up_ready = sem("up_ready")
        gelu_done = sem("gelu_done")
        act_split = sem("act_split")
        y_ready = sem("y_ready")
        y_out = sem("y_out")
        y_stored = sem("y_stored")
        w1_e = w1.rearrange("e (k p) f -> e p k f", p=P)
        w2_e = w2.rearrange("e (f p) d -> e p f d", p=P)
        xb_e = xbuf[0:SLOTS, :].rearrange("(e s p) d -> e p s d", p=P, s=ET)
        yb_e = ybuf.rearrange("(e s p) d -> e p s d", p=P, s=ET)
        R3, E8, S6 = (0, 1, 2), tuple(range(FT)), tuple(range(ET))

        def past(t, u, events, k):
            return 2 * len(events) * t + ((u + 1) * len(events) + events.index(k) + 1)

        def experts(body, eng):
            with eng.Fori(0, E // 2 - 1) as t:
                for u in range(2):
                    body(t, u, True)
            body(E // 2 - 1, 0, True)
            body(E // 2 - 1, 1, False)

        with nc.Block() as block:
            @block.sync
            def _(sp):
                def load(e, u):
                    one_e = lambda a: (a[bass.ds(e, 1)] if not isinstance(e, int) else a[e:e + 1]).rearrange("a p k f -> p (a k) f")
                    sp.dma_start(xb[:, u, :, :], one_e(xb_e)).then_inc(w_in[u], 16)
                    sp.dma_start(w1f[:, u, :, :], one_e(w1_e)).then_inc(w_in[u], 16)
                    sp.dma_start(w2f[:, u, :, :], one_e(w2_e)).then_inc(w_in[u], 16)

                def load_b2(e, u):
                    row = b2[bass.ds(e, 1), :] if not isinstance(e, int) else b2[e:e + 1, :]
                    sp.dma_start(b2w[:, u, :], row.broadcast_to([P, D])).then_inc(b2_in[u], 16)

                def store(t, u):
                    e = 2 * t + u
                    sp.wait_ge(y_out, past(t, u, S6, 5))
                    dst = (yb_e[bass.ds(e, 1)] if not isinstance(e, int) else yb_e[e:e + 1]).rearrange("a p k f -> p (a k) f")
                    sp.dma_start(dst, yo[:, u, :, :]).then_inc(y_stored, 16)

                sp.sem_inc(y_stored, 1)
                for u in range(2):
                    load(u, u)
                    load_b2(u, u)
                with sp.Fori(0, E // 2 - 1) as t:
                    for u in range(2):
                        wait_apart(sp, (split_w, past(t, u, R3, 2)))
                        sp.wait_ge(split_v, past(t, u, (0, 1), 1))
                        sp.wait_ge(xt_ready, past(t, u, R3, 2))
                        load(2 * t + 2 + u, u)
                        store(t, u)
                        load_b2(2 * t + 2 + u, u)
                for u in range(2):
                    store(E // 2 - 1, u)
                sp.wait_ge(y_stored, 16 * E + 1)

            @block.gpsimd
            def _(pool):
                def split(t, u):
                    t_, u_ = (t, u) if u < 2 else (t + 1, u - 2)
                    wait_apart(pool, (y_ready, past(t, u - 2, S6, 5)), (w_in[u % 2], 48 * (t_ + 1)))
                    nc.gpsimd.tensor_scalar(w1h[:, u % 2], w1f[:, u % 2], 1.0, 1.0, ALU.mult, ALU.mult).then_inc(split_w, 1)
                    nc.gpsimd.tensor_scalar(w2h[:, u % 2], w2f[:, u % 2], 1.0, 1.0, ALU.mult, ALU.mult).then_inc(split_w, 1)
                    pool.wait_ge(split_w, past(t, u, R3, 1))
                    nc.gpsimd.tensor_tensor(w2l[:, u % 2], w2f[:, u % 2], w2h[:, u % 2], ALU.subtract).then_inc(split_w, 1)

                pool.sem_inc(split_w, 3)
                split(0, 0)

                def body(t, u, more):
                    if more:
                        split(t, u + 1)

                experts(body, pool)

            @block.scalar
            def _(ac):
                def rows_high(t, u):
                    for r in R3:
                        ac.wait_ge(xt_ready, past(t, u, R3, r))
                        nc.scalar.activation(xh[:, u % 2, r * HALF:(r + 1) * HALF], xt_ps[r % 2][:], ACT.Copy).then_inc(xh_done, 1)

                def body(t, u, more):
                    for f in E8:
                        ac.wait_ge(up_ready, past(t, u, E8, f))
                        if f == 0:
                            ac.wait_ge(split_v, past(t, u, (0, 1), 1))
                        pu, pf = (u, f - 2) if f >= 2 else (u - 1, f + 6)
                        ac.wait_ge(act_split, past(t, pu, tuple(range(2 * FT)), 2 * pf + 1))
                        nc.scalar.activation(act_f[:, f % 2, :].rearrange("p (n c) -> p n c", n=2), g_ps4[f % 2][:, :, 0:NW],
                                             ACT.Gelu, bias=b1c[:, u, f:f + 1]).then_inc(gelu_done, 1)
                    if more:
                        rows_high(t, u + 1)

                for sm, n in ((xh_done, 3), (gelu_done, FT)):
                    ac.sem_inc(sm, n)
                rows_high(0, 0)
                experts(body, ac)

            @block.vector
            def _(v):
                def prepare(t, u):
                    t_, u_ = (t, u) if u < 2 else (t + 1, u - 2)
                    e = 2 * t + u
                    v.wait_ge(split_w, past(t, u, R3, 0))
                    nc.vector.tensor_tensor(w1l[:, u % 2], w1f[:, u % 2], w1h[:, u % 2], ALU.subtract).then_inc(split_v, 1)
                    v.wait_ge(gelu_done, past(t, u - 2, E8, 7))
                    src = b1T[:, bass.ds(e, 1), :] if not isinstance(e, int) else b1T[:, e:e + 1, :]
                    nc.vector.tensor_copy(b1c[:, u % 2, :], src.rearrange("p a f -> p (a f)")).then_inc(split_v, 1)

                def rows_low(t, u):
                    for r in R3:
                        v.wait_ge(xh_done, past(t, u, R3, r))
                        at = slice(r * HALF, (r + 1) * HALF)
                        nc.vector.tensor_tensor(xl[:, u % 2, at], xt_ps[r % 2][:], xh[:, u % 2, at], ALU.subtract).then_inc(xl_done, 1)

                def body(t, u, more):
                    steps = tuple(range(2 * FT))
                    for f in E8:
                        v.wait_ge(gelu_done, past(t, u, E8, f))
                        nc.vector.tensor_copy(act_h[:, f, :], act_f[:, f % 2, :]).then_inc(act_split, 1)
                        v.wait_ge(act_split, past(t, u, steps, 2 * f))
                        nc.vector.tensor_tensor(act_l[:, f, :], act_f[:, f % 2, :], act_h[:, f, :], ALU.subtract).then_inc(act_split, 1)
                    if more:
                        rows_low(t, u + 1)
                        prepare(t, u + 1)
                    v.wait_ge(b2_in[u], 16 * (t + 1))
                    v.wait_ge(y_stored, 32 * t + 1)
                    for s in S6:
                        v.wait_ge(y_ready, past(t, u, S6, s))
                        nc.vector.tensor_tensor(yo[:, u, s, :], y_ps[s % 2][:, 0:D], b2w[:, u, :], ALU.add).then_inc(y_out, 1)

                for sm, n in ((split_v, 2), (xl_done, 3), (act_split, 2 * FT), (y_out, ET)):
                    v.sem_inc(sm, n)
                rows_low(0, 0)
                prepare(0, 0)
                experts(body, v)

            @block.tensor
            def _(te):
                mm = nc.tensor.matmul

                def turn(t, u):
                    t_, u_ = (t, u) if u < 2 else (t + 1, u - 2)
                    te.wait_ge(w_in[u % 2], 48 * (t_ + 1))
                    for r in R3:
                        pu, pr = (u, r - 2) if r >= 2 else (u - 1, r + 1 if r else 2)
                        te.wait_ge(xl_done, past(t, u, R3, r - 2) if r >= 2 else past(t, u - 1, R3, 2))
                        for n in range(4 * r, 4 * r + 4):
                            k, s = n // ET, n % ET
                            last = nc.tensor.transpose(xt_ps[r % 2][:, (n % 4) * P:(n % 4 + 1) * P],
                                                       xb[:, u % 2, s, k * P:(k + 1) * P], ident[:])
                        last.then_inc(xt_ready, 1)

                def body(t, u, more):
                    te.wait_ge(xl_done, past(t, u, R3, 2))
                    te.wait_ge(split_w, past(t, u, R3, 2))
                    te.wait_ge(split_v, past(t, u, (0, 1), 0))
                    for f in E8:
                        pu, pf = (u, f - 2) if f >= 2 else (u - 1, f + 6)
                        te.wait_ge(gelu_done, past(t, pu, E8, pf))
                        for w, x, i in ((w1h, xh, 0), (w1h, xl, 1), (w1l, xh, 2)):
                            for k in range(KD):
                                for n in range(2):
                                    last = mm(g_ps4[f % 2][:, n, 0:NW], w[:, u, k, f * P:(f + 1) * P],
                                              x[:, u, k * CAP + n * NW:k * CAP + (n + 1) * NW],
                                              start=i == 0 and k == 0, stop=i == 2 and k == KD - 1)
                        last.then_inc(up_ready, 1)
                    if more:
                        turn(t, u + 1)
                    for s in S6:
                        te.wait_ge(y_out, past(t, u, S6, s - 2) if s >= 2 else past(t, u - 1, S6, s + 4))
                        for f in E8:
                            if s == 0:
                                te.wait_ge(act_split, past(t, u, tuple(range(2 * FT)), 2 * f + 1))
                            for x, w, i in ((act_h, w2h, 0), (act_h, w2l, 1), (act_l, w2h, 2)):
                                last = mm(y_ps[s % 2][:, 0:D], x[:, f, s * P:(s + 1) * P], w[:, u, f, :],
                                          start=i == 0 and f == 0, stop=i == 2 and f == FT - 1)
                        last.then_inc(y_ready, 1)

                for sm, n in ((xt_ready, 3), (up_ready, FT), (y_ready, ET)):
                    te.sem_inc(sm, n)
                turn(0, 0)
                experts(body, te)
        four.close()

        five = ExitStack()
        yg = sb(five, "yg", [P, 2, ST, D])
        from_slot = sb(five, "from_slot", [P, 2, ST], u32)
        gate = sb(five, "gate", [P, 2, ST])
        picked_s = sem("picked_s")
        gathered = [sem(f"gathered{n}") for n in range(2)]
        gated = sem("gated")
        stored = [sem(f"stored{n}") for n in range(2)]
        with nc.Block() as block:
            @block.gpsimd
            def _(pool):
                with pool.Fori(0, B // 2) as t:
                    for u in range(2):
                        wait_apart(pool, (picked_s, 4 * t + 2 * u + 2), (stored[u], 16 * t + 1))
                        for n in range(ST):
                            nc.gpsimd.indirect_dma_start(
                                out=yg[:, u, n, :], out_offset=None, in_=ybuf,
                                in_offset=bass.IndirectOffsetOnAxis(ap=from_slot[:, u, n:n + 1], axis=0)).then_inc(gathered[u], 16)

            @block.vector
            def _(v):
                def pick(t, u):
                    at = bass.ds((2 * t + u) * ST, ST)
                    nc.vector.tensor_copy(from_slot[:, u, :], slot_of[:, at]).then_inc(picked_s, 1)
                    nc.vector.tensor_copy(gate[:, u, :], gate_of[:, at]).then_inc(picked_s, 1)

                with v.Fori(0, B // 2) as t:
                    for u in range(2):
                        pick(t, u)
                    for u in range(2):
                        v.wait_ge(gathered[u], 16 * ST * (t + 1))
                        v.wait_ge(picked_s, 4 * t + 4)
                        for n in range(ST):
                            b = 2 * t + u
                            nc.vector.scalar_tensor_tensor(yg[:, u, n, :], yg[:, u, n, :], gate[:, u, n:n + 1],
                                                           mod[:, bass.ds(b, 1), GB, :].rearrange("p a d -> p (a d)"),
                                                           ALU.mult, ALU.mult).then_inc(gated, 1)
                            v.wait_ge(gated, 4 * ST * t + (2 * ST * u + 2 * n + 1))
                            nc.vector.tensor_tensor(yg[:, u, n, :], yg[:, u, n, :],
                                                    x1[:, bass.ds(b * ST + n, 1), :].rearrange("p a d -> p (a d)"),
                                                    ALU.add).then_inc(gated, 1)

            @block.sync
            def _(sp):
                for u in range(2):
                    sp.sem_inc(stored[u], 1)
                with sp.Fori(0, B // 2) as t:
                    for u in range(2):
                        sp.wait_ge(gated, 4 * ST * t + 2 * ST * (u + 1))
                        sp.dma_start(out_tiles[:, bass.ds((2 * t + u) * ST, ST), :], yg[:, u, :, :]).then_inc(stored[u], 16)
                for u in range(2):
                    sp.wait_ge(stored[u], 16 * (B // 2) + 1)
        five.close()


NAMES = ["L0_attn_" + n for n in ("h_t", "W_DQ", "b_DQ", "W_UQ", "b_UQ", "W_DKV", "b_DKV", "W_UK", "b_UK", "W_UV",
                                  "b_UV", "W_QR", "b_QR", "W_KR", "b_KR", "W_O", "b_O")]
NAMES += ["L0_ffn_router_w", "L0_ffn_w1", "L0_ffn_b1", "L0_ffn_w2", "L0_ffn_b2", "L0_c", "L0_wmod"]


def kernel(**inputs):
    import concourse.bacc as bacc
    from concourse.bass_utils import run_bass_kernel_spmd

    nc = bacc.Bacc("TRN2", target_bir_lowering=False, num_devices=1)
    arrays, args = {}, []
    for name in NAMES:
        a = np.ascontiguousarray(inputs[name])
        arrays["in_" + name] = a
        args.append(nc.dram_tensor("in_" + name, a.shape, mybir.dt.from_np(a.dtype), kind="ExternalInput").ap())
    result = nc.dram_tensor("out_0", (B, S, D), fp32, kind="ExternalOutput").ap()
    adaln_block(nc, *args, result)
    r = run_bass_kernel_spmd(nc, [arrays], core_ids=[0])
    return r.results[0]["out_0"]
```

```python
from contextlib import ExitStack

import numpy as np
import concourse.bass as bass
from concourse import mybir

fp32 = mybir.dt.float32
fp16 = mybir.dt.float16
i32 = mybir.dt.int32
u32 = mybir.dt.uint32
ALU = mybir.AluOpType
ACT = mybir.ActivationFunctionType
AX = mybir.AxisListType

P = 128
B, S, D = 4, 1024, 256
H, DK, DC, DR = 8, 128, 32, 32
E, F = 8, 1024
N = B * S
CAP = -(-3 * N // (2 * E))
KD = D // P
ST = S // P
NT = N // P
SLOTS = E * CAP
ET = CAP // P
FT = F // P
HALF = 512
LR = DC + DR
QROWS = 3 * DC + 2
SCALE = float(DK + DR) ** -0.5
EPS = 1e-5

VC = 2 * DC + 1
VP = 2 * DC + 2
ALL = tuple(range(8))
CAST_ACT = (0, 1, 2, 3, 6, 7)
CAST_DVE = (4, 5)
CAST_POOL = ()
SUB_POOL = (0, 1, 2, 3, 5, 6, 7)
SUB_DVE = (4,)


def adaln_block(nc, h_t, W_DQ, b_DQ, W_UQ, b_UQ, W_DKV, b_DKV, W_UK, b_UK, W_UV, b_UV, W_QR, b_QR,
                W_KR, b_KR, W_O, b_O, router_w, w1, b1, w2, b2, c, wmod, out):
    x_tiles = h_t.rearrange("b (t p) d -> p (b t) d", p=P)
    out_tiles = out.rearrange("b (t p) d -> p (b t) d", p=P)
    xbuf = nc.dram_tensor("xbuf", [SLOTS + P, D], fp32).ap()
    ybuf = nc.dram_tensor("ybuf", [SLOTS, D], fp32).ap()

    ctx = ExitStack()
    with ctx:
        def sem(name):
            return ctx.enter_context(nc.semaphore(name))

        def sb(scope, name, shape, dt=fp32):
            return scope.enter_context(nc.sbuf_tensor(name, shape, dt))

        def ps(scope, name, shape, dt=fp32):
            return scope.enter_context(nc.psum_tensor(name, shape, dt))

        ident = sb(ctx, "ident", [P, P])
        ident16 = sb(ctx, "ident16", [P, P], fp16)
        upto16 = sb(ctx, "upto16", [P, P], fp16)
        ones16 = sb(ctx, "ones16", [P, P], fp16)
        mod = sb(ctx, "mod", [P, B, 4, D])
        GA, SB_, CB, GB = range(4)
        proj = sb(ctx, "proj", [P, KD, D])
        attn_bias = sb(ctx, "attn_bias", [P, D])
        cols = sb(ctx, "cols", [P, 96])
        b1T = cols[:, 0:64].rearrange("p (e f) -> p e f", e=E)
        rwT = cols[:, 64:80].rearrange("p (e k) -> p k e", e=E)
        rev = sb(ctx, "rev", [P, E])
        first_slot = sb(ctx, "first_slot", [P, E])
        trash = sb(ctx, "trash", [P, 1])
        minus_half = sb(ctx, "minus_half", [P, ST])
        x1 = sb(ctx, "x1", [P, NT, D])
        slot_of = sb(ctx, "slot_of", [P, NT], u32)
        gate_of = sb(ctx, "gate_of", [P, NT])

        zeroed = sem("zeroed")

        const_v = sem("const_v")

        def wait_apart(eng, *waits):
            waits = [(sm, value if isinstance(value, int) else eng.compute_val(value)) for sm, value in waits]
            eng.wait_ge(const_v, 1)
            for sm, value in waits:
                eng.wait_ge(sm, value)

        inner = ExitStack()
        KA = sb(inner, "KA", [P, N], fp16)
        KB = sb(inner, "KB", [LR + 2, N], fp16)
        CQ = sb(inner, "CQ", [QROWS, N], fp16)
        VV = sb(inner, "VV", [P, NT, VP], fp16)
        GQ = sb(inner, "GQ", [QROWS, H, P], fp16)
        mz = sb(inner, "mz", [P, ST, LR + 2], fp16)

        one = ExitStack()
        xs = x1
        wk = sb(one, "wk", [P, KD, P])
        wq = sb(one, "wq", [P, KD, 3 * DC])
        bk = sb(one, "bk", [P, 1])
        bq = sb(one, "bq", [3 * DC, 1])
        uq = sb(one, "uq", [QROWS, H * DK])
        qr = sb(one, "qr", [QROWS, H, DR])
        ukv = sb(one, "ukv", [2 * DC, H * DK])
        rows = sb(one, "rows", [96, P])
        wo = sb(one, "wo", [DK, H, D])
        bo = sb(one, "bo", [1, D])
        wm = sb(one, "wm", [P, KD, 6 * D])
        iota_i = sb(one, "iota_i", [P, 2 * E + 1], i32)
        silc = sb(one, "silc", [P, B, KD])
        silrep = sb(one, "silrep", [P, B, KD, P])
        bvrep = sb(one, "bvrep", [P, H, P])
        onesrow = sb(one, "onesrow", [1, P])
        shiftT = sb(one, "shiftT", [P, 4, B])
        uqT = sb(one, "uqT", [P, H, P])
        ukvT = sb(one, "ukvT", [P, H, 2 * DC])
        G = sb(one, "G", [QROWS, H, P])
        zeros = sb(one, "zeros", [P, 7 * D])
        stats = sb(one, "stats", [P, ST, 6])
        mv = sb(one, "mv", [P, ST, 2])
        vare = sb(one, "vare", [P, ST])
        rstd = sb(one, "rstd", [P, ST])
        xn = sb(one, "xn", [P, ST, D])
        hT = sb(one, "hT", [P, KD, S])
        sign = sb(one, "sign", [P, 2, D])
        size = sb(one, "size", [P, 2, D])

        t_ps = [ps(one, f"t_ps{n}", [P, HALF]) for n in range(3)]
        k_ps = ps(one, "k_ps", [P, S])
        q_ps = ps(one, "q_ps", [P, S])
        v_ps = ps(one, "v_ps", [P, ST, P], fp16)

        x_in = [sem(f"x_in{b}") for b in range(B)]
        rows_in = sem("rows_in")
        shift_in = sem("shift_in")
        up_in = sem("up_in")
        latent_in = sem("latent_in")
        gates_in = sem("gates_in")
        wo_in = sem("wo_in")
        const_p = sem("const_p")
        turned_rows = sem("turned_rows")
        cols_done = sem("cols_done")
        silu_done = sem("silu_done")
        shift_ready = sem("shift_ready")
        shift_done = sem("shift_done")
        side_ready = sem("side_ready")
        side_done = sem("side_done")
        prep = sem("prep")
        gate_steps = sem("gate_steps")
        ln_v = sem("ln_v")
        ln_var = sem("ln_var")
        ln_rstd = sem("ln_rstd")
        ln_xn = sem("ln_xn")
        xT_ready = sem("xT_ready")
        hT_ready = sem("hT_ready")
        kq_ready = sem("kq_ready")
        hi_done = sem("hi_done")
        lo_done = sem("lo_done")
        v_ready = sem("v_ready")
        v_done = sem("v_done")
        SIDE = 7 + 2 * B

        with nc.Block() as block:
            @block.sync
            def _(sp):
                def load(dst, src, sm):
                    sp.dma_start(dst, src).then_inc(sm, 16)

                def load_x(b):
                    load(xs[:, b * ST:(b + 1) * ST, :], x_tiles[:, b * ST:(b + 1) * ST, :], x_in[b])

                load(rows[0:64, :], b1.rearrange("e (f p) -> (e f) p", p=P), rows_in)
                load(rows[64:80, :], router_w.rearrange("e (k p) -> (e k) p", p=P), rows_in)
                load_x(0)
                wm_k = wmod.rearrange("(k p) n -> p k n", p=P)
                load(wm[:, :, 0:2 * D], wm_k[:, :, 0:2 * D], shift_in)
                for r in range(3):
                    load(uq[r * DC:(r + 1) * DC, :], W_UQ, up_in)
                    load(qr[r * DC:(r + 1) * DC, :, :], W_QR.rearrange("c (h r) -> c h r", r=DR), up_in)
                for r in range(2):
                    row = b_UQ.rearrange("(a n) -> a n", a=1)
                    load(uq[3 * DC + r:3 * DC + r + 1, :], row, up_in)
                    load(qr[3 * DC + r:3 * DC + r + 1, :, :], b_QR.rearrange("(a h r) -> a h r", a=1, r=DR), up_in)
                load(ukv[0:DC, :], W_UK, up_in)
                load(ukv[DC:2 * DC, :], W_UV, up_in)
                load_x(1)
                load(wo[:], W_O.rearrange("(h d) n -> d h n", d=DK), wo_in)
                load(bo[:], b_O.rearrange("(a n) -> a n", a=1), wo_in)
                load(wm[:, :, 2 * D:6 * D], wm_k[:, :, 2 * D:6 * D], gates_in)
                load_x(2)
                load_x(3)
                sp.wait_ge(const_v, 1)
                for n in range((SLOTS + P) // (7 * P)):
                    sp.dma_start(xbuf[n * 7 * P:(n + 1) * 7 * P, :].rearrange("(p r) d -> p (r d)", p=P),
                                 zeros[:]).then_inc(zeroed, 16)
                sp.wait_ge(zeroed, 16 * ((SLOTS + P) // (7 * P)))

            @block.scalar
            def _(ac):
                def load(dst, src, sm):
                    ac.dma_start(dst, src).then_inc(sm, 16)

                load(rows[80:88, :], c.rearrange("b (k p) -> (b k) p", p=P), rows_in)
                load(rows[88:96, :], b_UV.rearrange("(h d) -> h d", d=DK), rows_in)
                for r in range(2):
                    load(wk[:, :, r * LR:r * LR + DC], W_DKV.rearrange("(k p) n -> p k n", p=P), latent_in)
                    load(wk[:, :, r * LR + DC:(r + 1) * LR], W_KR.rearrange("(k p) n -> p k n", p=P), latent_in)
                    load(bk[r * LR:r * LR + DC, :], b_DKV.rearrange("(p a) -> p a", a=1), latent_in)
                    load(bk[r * LR + DC:(r + 1) * LR, :], b_KR.rearrange("(p a) -> p a", a=1), latent_in)
                for r in range(3):
                    load(wq[:, :, r * DC:(r + 1) * DC], W_DQ.rearrange("(k p) n -> p k n", p=P), latent_in)
                    load(bq[r * DC:(r + 1) * DC, :], b_DQ.rearrange("(p a) -> p a", a=1), latent_in)

                ac.wait_ge(cols_done, 1)
                nc.scalar.activation(silc[:], cols[:, 80:88].rearrange("p (b k) -> p b k", k=KD),
                                     ACT.Silu).then_inc(silu_done, 1)

                def features(b):
                    if b == 0:
                        ac.wait_ge(shift_done, 2)
                    else:
                        ac.wait_ge(kq_ready, 2 * b)
                    for g in range(2):
                        for k in range(KD):
                            n = 4 * b + 2 * g + k
                            ac.wait_ge(xT_ready, n + 1)
                            nc.scalar.activation(hT[:, k, g * HALF:(g + 1) * HALF], t_ps[n % 2][:],
                                                 ACT.Identity, scale=shiftT[:, 2 + k, b:b + 1],
                                                 bias=shiftT[:, k, b:b + 1]).then_inc(hT_ready, 1)

                features(0)
                for b in range(B):
                    if b == 0:
                        ac.wait_ge(latent_in, 16 * 14)
                    ac.wait_ge(kq_ready, 2 * b + 1)
                    nc.scalar.activation(KA[:, b * S:(b + 1) * S], k_ps[:], ACT.Identity, bias=bk[:]).then_inc(hi_done, 1)
                    ac.wait_ge(kq_ready, 2 * b + 2)
                    nc.scalar.activation(CQ[0:3 * DC, b * S:(b + 1) * S], q_ps[0:3 * DC, :], ACT.Identity,
                                         bias=bq[:]).then_inc(hi_done, 1)
                    if b + 1 < B:
                        features(b + 1)

            @block.gpsimd
            def _(pool):
                nc.gpsimd.memset(ident[:], 0.0).then_inc(const_p, 1)
                nc.gpsimd.memset(ident16[:], 0.0).then_inc(const_p, 1)
                nc.gpsimd.memset(upto16[:], 1.0).then_inc(const_p, 1)
                pool.wait_ge(const_p, 3)
                for m in (ident, ident16):
                    nc.gpsimd.affine_select(out=m[:], in_=m[:], compare_op=ALU.not_equal, fill=1.0, base=0,
                                            pattern=[[-1, P]], channel_multiplier=1).then_inc(const_p, 1)
                nc.gpsimd.affine_select(out=upto16[:], in_=upto16[:], compare_op=ALU.is_ge, fill=0.0, base=0,
                                        pattern=[[1, P]], channel_multiplier=-1).then_inc(const_p, 1)
                nc.gpsimd.iota(iota_i[:, 0:E], pattern=[[-1, E]], base=E, channel_multiplier=0).then_inc(const_p, 1)
                nc.gpsimd.iota(iota_i[:, E:2 * E], pattern=[[CAP, E]], base=0, channel_multiplier=0).then_inc(const_p, 1)
                nc.gpsimd.iota(iota_i[:, 2 * E:2 * E + 1], pattern=[[0, 1]], base=SLOTS, channel_multiplier=1).then_inc(const_p, 1)
                fills = ((ones16[:], 1.0), (onesrow[:], 1.0), (mz[:], 0.0), (VV[:, :, 2 * DC:VP], 1.0),
                         (KB[LR:LR + 2, :], -1.0), (CQ[3 * DC:QROWS, :], 1.0))
                for n, (dst, value) in enumerate(fills):
                    pool.wait_ge(const_p, 9 + n)
                    nc.gpsimd.memset(dst, value).then_inc(const_p, 1)
                pool.wait_ge(const_p, 15)
                pool.wait_ge(const_v, 2)
                for b in range(B):
                    pool.wait_ge(ln_var, b + 1)
                    nc.gpsimd.tensor_tensor(rstd[:], vare[:], minus_half[:], ALU.pow).then_inc(ln_rstd, 1)

            @block.vector
            def _(v):
                nc.vector.memset(zeros[:], 0.0).then_inc(const_v, 1)
                nc.vector.memset(minus_half[:], -0.5).then_inc(const_v, 1)

                def spread(b):
                    v.wait_ge(x_in[b], 16)
                    for t in range(ST):
                        nc.vector.bn_stats(stats[:, t, :], xs[:, b * ST + t, :]).then_inc(ln_v, 1)
                    v.wait_ge(ln_v, b * (2 * ST) + ST)
                    for t in range(ST):
                        nc.vector.bn_aggr(mv[:, t, :], stats[:, t, :]).then_inc(ln_v, 1)
                    v.wait_ge(ln_v, (b + 1) * (2 * ST))
                    nc.vector.tensor_scalar(vare[:], mv[:, :, 1], EPS, None, ALU.add).then_inc(ln_var, 1)

                def normalise(b):
                    v.wait_ge(ln_rstd, b + 1)
                    if b:
                        v.wait_ge(xT_ready, 4 * b)
                    for t in range(ST):
                        nc.vector.tensor_scalar(xn[:, t, :], xs[:, b * ST + t, :], mv[:, t, 0:1],
                                                rstd[:, t:t + 1], ALU.subtract, ALU.mult).then_inc(ln_xn, 1)

                def side_out(n):
                    v.wait_ge(side_ready, n + 1)
                    bank = t_ps[2]
                    if n < 2:
                        nc.vector.tensor_copy(uqT[:, 4 * n:4 * n + 4, 0:QROWS],
                                              bank[:].rearrange("p (h c) -> p h c", h=4)[:, :, 0:QROWS]).then_inc(side_done, 1)
                    elif n == 2:
                        nc.vector.tensor_copy(ukvT[:], bank[:].rearrange("p (h c) -> p h c", h=H)).then_inc(side_done, 1)
                    elif n == 3:
                        g_ps = bank[0:QROWS, 0:H * DC].rearrange("p (h c) -> p h c", h=H)
                        nc.vector.tensor_scalar(G[:, :, 0:DC], g_ps, SCALE, None, ALU.mult).then_inc(prep, 1)
                        nc.vector.tensor_scalar(G[:, :, LR:LR + DC], g_ps, SCALE, None, ALU.mult).then_inc(side_done, 1)
                        for r in range(2):
                            nc.vector.tensor_scalar(G[:, :, r * LR + DC:(r + 1) * LR], qr[:], SCALE, None, ALU.mult).then_inc(prep, 1)
                        v.wait_ge(prep, 3)
                        v.wait_ge(side_done, 4)
                        nc.vector.tensor_copy(GQ[:], G[:]).then_inc(prep, 1)
                        v.wait_ge(prep, 4)
                        nc.vector.tensor_tensor(GQ[64:QROWS, :, :], G[64:QROWS, :, :], GQ[64:QROWS, :, :], ALU.subtract).then_inc(prep, 1)
                        v.wait_ge(prep, 5)
                        nc.vector.tensor_copy(GQ[96:97, :, :], G[96:97, :, :]).then_inc(prep, 1)
                    elif n < 6:
                        nc.vector.tensor_copy(proj[:, n - 4, :], bank[:, 0:D]).then_inc(side_done, 1)
                    elif n == 6:
                        nc.vector.tensor_copy(attn_bias[:], bank[:, 0:D]).then_inc(side_done, 1)
                    else:
                        b, half = (n - 7) // 2, (n - 7) % 2
                        nc.vector.tensor_copy(mod[:, b, 2 * half:2 * half + 2, :],
                                              bank[:].rearrange("p (m d) -> p m d", m=2)).then_inc(side_done, 1)
                        if half:
                            v.wait_ge(side_done, n + 1)
                            g = mod[:, b, 0:4:3, :]
                            nc.vector.tensor_scalar(sign[:], g, 0.0, 2.0, ALU.is_ge, ALU.mult).then_inc(gate_steps, 1)
                            nc.vector.scalar_tensor_tensor(size[:], g, -1.0, g, ALU.mult, ALU.max).then_inc(gate_steps, 1)
                            v.wait_ge(gate_steps, 5 * b + 2)
                            nc.vector.tensor_scalar(g, size[:], 0.25, None, ALU.max).then_inc(gate_steps, 1)
                            v.wait_ge(gate_steps, 5 * b + 3)
                            nc.vector.scalar_tensor_tensor(g, sign[:], -1.0, g, ALU.add, ALU.mult).then_inc(gate_steps, 1)
                            nc.vector.tensor_scalar(mod[:, b, CB, :], mod[:, b, CB, :], 1.0, None, ALU.add).then_inc(gate_steps, 1)
                            v.wait_ge(gate_steps, 5 * b + 5)

                v.wait_ge(turned_rows, 1)
                nc.vector.tensor_copy(cols[:], t_ps[0][:, 0:96]).then_inc(cols_done, 1)
                spread(0)
                normalise(0)
                v.wait_ge(shift_ready, 1)
                nc.vector.tensor_copy(shiftT[:, 0:2, :], t_ps[1][:, 0:2 * B].rearrange("p (m b) -> p m b", b=B)).then_inc(shift_done, 1)
                nc.vector.tensor_scalar(shiftT[:, 2:4, :], t_ps[1][:, 2 * B:4 * B].rearrange("p (m b) -> p m b", b=B),
                                        1.0, None, ALU.add).then_inc(shift_done, 1)
                v.wait_ge(cols_done, 1)
                nc.vector.tensor_copy(bvrep[:], cols[:, 88:96].unsqueeze(2).broadcast_to([P, H, P])).then_inc(cols_done, 1)
                v.wait_ge(silu_done, 1)
                nc.vector.tensor_copy(silrep[:], silc[:].unsqueeze(3).broadcast_to([P, B, KD, P])).then_inc(cols_done, 1)
                v.wait_ge(const_p, 9)
                nc.vector.tensor_copy(rev[:], iota_i[:, 0:E])
                nc.vector.tensor_copy(first_slot[:], iota_i[:, E:2 * E])
                nc.vector.tensor_copy(trash[:], iota_i[:, 2 * E:2 * E + 1])

                for b in range(B):
                    side_out(4 * b)
                    side_out(4 * b + 1)
                    if b + 1 < B:
                        spread(b + 1)
                    side_out(4 * b + 2)
                    if b + 1 < B:
                        normalise(b + 1)
                    if 4 * b + 3 < SIDE:
                        side_out(4 * b + 3)
                    v.wait_ge(hi_done, 2 * b + 1)
                    at = slice(b * S, (b + 1) * S)
                    nc.vector.scalar_tensor_tensor(KA[LR:P, at], k_ps[LR:P, :], bk[LR:P, :], KA[LR:P, at],
                                                   ALU.add, ALU.subtract).then_inc(lo_done, 1)
                    v.wait_ge(hi_done, 2 * b + 2)
                    nc.vector.scalar_tensor_tensor(CQ[DC:2 * DC, at], q_ps[DC:2 * DC, :], bq[DC:2 * DC, :],
                                                   CQ[DC:2 * DC, at], ALU.add, ALU.subtract).then_inc(lo_done, 1)
                    nc.vector.tensor_copy(KB[0:LR, at], KA[0:LR, at])
                    v.wait_ge(v_ready, b + 1)
                    for low in range(2):
                        nc.vector.tensor_copy(VV[:, b * ST:(b + 1) * ST, (1 - low) * DC:(2 - low) * DC],
                                              v_ps[:, :, low * LR:low * LR + DC]).then_inc(v_done, 1)

            @block.tensor
            def _(te):
                mm = nc.tensor.matmul

                def turn(b):
                    for g in range(2):
                        te.wait_ge(ln_xn, b * ST + 4 * g + 4)
                        for k in range(KD):
                            n = 4 * b + 2 * g + k
                            if n >= 2:
                                te.wait_ge(hT_ready, n - 1)
                            for t in range(4):
                                last = nc.tensor.transpose(t_ps[n % 2][:, t * P:(t + 1) * P],
                                                           xn[:, 4 * g + t, k * P:(k + 1) * P], ident[:])
                            last.then_inc(xT_ready, 1)

                def latent(b, which):
                    if which == 0:
                        te.wait_ge(hT_ready, 4 * b + 4)
                    if b == 0:
                        te.wait_ge(latent_in, 16 * 14)
                    else:
                        te.wait_ge(lo_done, 2 * (b - 1) + which + 1)
                    o, w, m = ((k_ps, wk, P), (q_ps, wq, 3 * DC))[which]
                    for g in range(2):
                        for k in range(KD):
                            last = mm(o[0:m, g * HALF:(g + 1) * HALF], w[:, k, :], hT[:, k, g * HALF:(g + 1) * HALF],
                                      start=k == 0, stop=k == KD - 1)
                    last.then_inc(kq_ready, 1)

                def values(b):
                    te.wait_ge(lo_done, 2 * b + 1)
                    if b:
                        te.wait_ge(v_done, 2 * b)
                    for t in range(ST):
                        last = nc.tensor.transpose(v_ps[:, t, :], KA[:, b * S + t * P:b * S + (t + 1) * P], ident16[:])
                    last.then_inc(v_ready, 1)

                def side(n):
                    bank = t_ps[2]
                    if n:
                        te.wait_ge(side_done, n)
                    if n == 0:
                        te.wait_ge(up_in, 16 * 12)
                    if n == 4:
                        te.wait_ge(wo_in, 16 * 2)
                        te.wait_ge(cols_done, 2)
                    if n == 7:
                        te.wait_ge(gates_in, 16)
                        te.wait_ge(cols_done, 3)
                    if n < 2:
                        for h in range(4):
                            last = nc.tensor.transpose(bank[:, h * P:h * P + QROWS], uq[:, (4 * n + h) * DK:(4 * n + h + 1) * DK],
                                                       ident[0:QROWS, 0:QROWS])
                    elif n == 2:
                        for h in range(H):
                            last = nc.tensor.transpose(bank[:, h * 2 * DC:(h + 1) * 2 * DC], ukv[:, h * DK:(h + 1) * DK],
                                                       ident[0:2 * DC, 0:2 * DC])
                    elif n == 3:
                        for h in range(H):
                            last = mm(bank[0:QROWS, h * DC:(h + 1) * DC], uqT[:, h, 0:QROWS], ukvT[:, h, 0:DC], start=True, stop=True)
                    elif n < 6:
                        for h in range(4 * (n - 4), 4 * (n - 3)):
                            r = DC * (h % 4)
                            last = mm(bank[r:r + DC, 0:D], ukvT[:, h, DC:2 * DC], wo[:, h, :], start=True, stop=True)
                    elif n == 6:
                        for h in range(H):
                            mm(bank[:, 0:D], bvrep[:, h, :], wo[:, h, :], start=h == 0, stop=False)
                        last = mm(bank[:, 0:D], onesrow[:], bo[:], start=False, stop=True)
                    else:
                        b, half = (n - 7) // 2, (n - 7) % 2
                        for k in range(KD):
                            last = mm(bank[:], silrep[:, b, k, :], wm[:, k, (2 + 2 * half) * D:(4 + 2 * half) * D],
                                      start=k == 0, stop=k == KD - 1)
                    last.then_inc(side_ready, 1)

                te.wait_ge(const_p, 11)
                te.wait_ge(rows_in, 16 * 4)
                nc.tensor.transpose(t_ps[0][:, 0:96], rows[:], ident[0:96, 0:96]).then_inc(turned_rows, 1)
                te.wait_ge(silu_done, 1)
                te.wait_ge(shift_in, 16)
                for m in range(4):
                    for k in range(KD):
                        last = mm(t_ps[1][:, m * B:(m + 1) * B], wm[:, k, m * P:(m + 1) * P], silc[:, :, k],
                                  start=k == 0, stop=k == KD - 1)
                last.then_inc(shift_ready, 1)
                te.wait_ge(shift_done, 2)
                for b in range(B):
                    turn(b)
                    if b:
                        values(b - 1)
                    side(4 * b)
                    side(4 * b + 1)
                    latent(b, 0)
                    side(4 * b + 2)
                    latent(b, 1)
                    if 4 * b + 3 < SIDE:
                        side(4 * b + 3)
                values(B - 1)
        one.close()

        two = inner
        latents = ExitStack()
        o_n = latents.enter_context(nc.sbuf_tensor("o_n", [P, NT, D], fp32, side="right"))
        QA = sb(two, "QA", [P, 4, S], fp16)
        QB = sb(two, "QB", [LR + 2, 4, S], fp16)
        prob = sb(two, "prob", [P, 8, S])
        prob_hi = sb(two, "prob_hi", [P, 8, S], fp16)
        prob_lo = sb(two, "prob_lo", [P, 8, S], fp16)
        part_max = sb(two, "part_max", [P, ST, 2])
        row_max = sb(two, "row_max", [P, ST])
        raw = sb(two, "raw", [P, ST, VC])
        rsum = sb(two, "rsum", [P, ST])
        both = sb(two, "both", [P, ST, DC])
        st_ps = [ps(two, f"st_ps{n}", [P, S]) for n in range(2)]
        acc_ps = ps(two, "acc_ps", [P, ST, P])
        x_ps = [ps(two, f"x_ps{n}", [P, HALF]) for n in range(2)]

        scores_ready = sem("scores_ready")
        exp_done = sem("exp_done")
        cast_done = [sem(f"cast_done{k}") for k in ALL]
        sub_done = [sem(f"sub_done{k}") for k in ALL]
        pv_done = sem("pv_done")
        smax_ready = sem("smax_ready")
        smax_done = sem("smax_done")
        q_ready = sem("q_ready")
        qa_done = sem("qa_done")
        ql_done = sem("ql_done")
        split_done = sem("split_done")
        mrow_ready = sem("mrow_ready")
        mrow_done = sem("mrow_done")
        raw_done = sem("raw_done")
        norm_done = sem("norm_done")
        norm_steps = sem("norm_steps")
        HALVES = (0, 1)
        SIXTEEN = tuple(range(16))
        STEPS = (0, 1, 2)
        ONCE = (0,)
        AHEAD = 4
        QUERY_SLOT = 3
        OTHERS = (
            ((), (13,), (14,), ()),
            ((15,), (), (), ()),
            ((), ("r0",), (), ("r1",)),
            (("q0",), ("q1",), (), ()),
            ((), (0,), (1,), (2,)),
            ((), (3,), (4,), ()),
            ((5,), (6,), (7,), ()),
            ((8,), (9,), (10, 11), (12,)),
        )
        DIVIDE_SLOT = 2

        def after(t, u, pair, k):
            events = pair[1]
            return 4 * len(events) * t + ((u + 1) * len(events) + events.index(k) + 1)

        def place(t, u):
            if u >= 4:
                t, u = (t + 1) & 7, u - 4
            if u < 0:
                t, u = (t + 7) & 7, u + 4
            b = t >> 1
            return (b if isinstance(t, int) else b.with_bounds(min_val=0, max_val=B - 1)), (t & 1) * 4 + u

        def ahead(u, k, n):
            return u + (k + n) // 8, (k + n) % 8

        def others(act, t, u, k, gaps=(0, 1, 2, 3)):
            for gap in gaps:
                for item in OTHERS[k][gap]:
                    act(t, u + 1 if k < QUERY_SLOT else u + 2, item)

        def slots(body, t, head_range, k_range=ALL):
            for u in head_range:
                for k in k_range:
                    body(t, u, k)

        with nc.Block() as block:
            @block.tensor
            def _(te):
                mm = nc.tensor.matmul

                def other(t, j, item):
                    b, h = place(t, j)
                    if item in ("q0", "q1"):
                        f = int(item[1])
                        te.wait_ge(mrow_done, after(t, j - 1, (0, HALVES), f))
                        mm(x_ps[f][:], GQ[:, bass.ds(h, 1), :].rearrange("p a c -> p (a c)"),
                           CQ[:, bass.ds(b * S + f * HALF, HALF)], start=True, stop=True).then_inc(q_ready, 1)
                    elif item in ("r0", "r1"):
                        f = int(item[1])
                        te.wait_ge(split_done, after(t, j, (0, STEPS), 2))
                        for q in range(4):
                            last = mm(x_ps[f][0:LR + 2, q * P:(q + 1) * P], mz[:, 4 * f + q, :], ident16[:],
                                      start=True, stop=True)
                        last.then_inc(mrow_ready, 1)
                    else:
                        q, f = item // 2, item % 2
                        if q == 0:
                            te.wait_ge(ql_done, after(t, j, (0, HALVES), f))
                        else:
                            te.wait_ge(smax_done, after(t, j, (0, SIXTEEN), item - 2))
                        mm(x_ps[f][:], QA[:, j % 4, q * P:(q + 1) * P], KA[:, bass.ds(b * S + f * HALF, HALF)],
                           start=True, stop=True).then_inc(smax_ready, 1)

                def scores(t, j, k, keys):
                    b, _ = place(t, j)
                    pj, pk = ahead(j, k, -2)
                    first = keys is KA
                    q, r = (QA, P) if first else (QB, LR + 2)
                    if k == 0 and not first:
                        te.wait_ge(ql_done, after(t, j, (0, HALVES), 1))
                        te.wait_ge(mrow_done, after(t, j, (0, HALVES), 1))
                    if first:
                        te.wait_ge(exp_done, after(t, pj, (0, ALL), pk))
                    for f in HALVES:
                        last = mm(st_ps[k % 2][:, f * HALF:(f + 1) * HALF], keys[0:r, bass.ds(b * S + k * P, P)],
                                  q[0:r, j % 4, f * HALF:(f + 1) * HALF], start=first, stop=not first)
                    if not first:
                        last.then_inc(scores_ready, 1)

                def values(t, u, k):
                    b, _ = place(t, u)
                    if k == 0:
                        te.wait_ge(raw_done, after(t, u - 1, (0, ONCE), 0))
                    te.wait_ge(cast_done[k], after(t, u, (0, ONCE), 0))
                    te.wait_ge(sub_done[k], after(t, u, (0, ONCE), 0))
                    for q in range(ST):
                        for part, c in ((prob_hi, 0), (prob_lo, DC)):
                            last = mm(acc_ps[:, q, c:VC], part[:, k, q * P:(q + 1) * P],
                                      VV[:, bass.ds(b * ST + k, 1), c:VC].rearrange("p a c -> p (a c)"),
                                      start=k == 0 and q % 4 == 0 and c == 0, stop=k == 7 and q % 4 == 3 and c > 0)
                    last.then_inc(pv_done, 1)

                def slot(t, u, k):
                    others(other, t, u, k, (0,))
                    scores(t, *ahead(u, k, AHEAD), KA)
                    others(other, t, u, k, (1,))
                    scores(t, *ahead(u, k, AHEAD), KB)
                    others(other, t, u, k, (2,))
                    values(t, u, k)
                    others(other, t, u, k, (3,))

                for sm, n in ((scores_ready, 8), (pv_done, 8), (smax_ready, 16), (q_ready, 2), (mrow_ready, 2)):
                    te.sem_inc(sm, n)
                for k in range(QUERY_SLOT, 8):
                    others(other, 0, -2, k)
                for k in ALL:
                    if k >= 8 - AHEAD:
                        for keys in (KA, KB):
                            scores(0, *ahead(-1, k, AHEAD), keys)
                    others(other, 0, -1, k)
                with te.Fori(0, B * H // 4) as t:
                    slots(slot, t, range(4))

            @block.scalar
            def _(ac):
                def exponentials(t, j, k):
                    ac.wait_ge(scores_ready, after(t, j, (0, ALL), k))
                    pj, pk = j - 1, k
                    ac.wait_ge(sub_done[k], after(t, pj, (0, ONCE), 0))
                    nc.scalar.activation(prob[:, k, :], st_ps[k % 2][:], ACT.Exp).then_inc(exp_done, 1)

                def other(t, j, item):
                    if item in ("q0", "q1"):
                        f = int(item[1])
                        ac.wait_ge(q_ready, after(t, j, (0, HALVES), f))
                        nc.scalar.activation(QA[:, j % 4, f * HALF:(f + 1) * HALF], x_ps[f][:], ACT.Copy).then_inc(qa_done, 1)
                    if item in ("r0", "r1"):
                        f = int(item[1])
                        ac.wait_ge(mrow_ready, after(t, j, (0, HALVES), f))
                        nc.scalar.activation(QB[LR:LR + 2, j % 4, f * HALF:(f + 1) * HALF], x_ps[f][LR:LR + 2, :],
                                             ACT.Copy).then_inc(mrow_done, 1)

                def round_probs(t, j, k):
                    pj, pk = j - 1, k
                    ac.wait_ge(exp_done, after(t, j, (0, ALL), k))
                    ac.wait_ge(pv_done, after(t, pj, (0, ALL), pk))
                    nc.scalar.activation(prob_hi[:, k, :], prob[:, k, :], ACT.Copy).then_inc(cast_done[k], 1)

                def ahead_part(t, u, k):
                    others(other, t, u, k, (0, 1, 2))
                    if k >= 8 - AHEAD or u >= 0:
                        exponentials(t, *ahead(u, k, AHEAD))
                    others(other, t, u, k, (3,))
                    j, kk = ahead(u, k, AHEAD - 1)
                    if j >= 0 and kk in CAST_ACT:
                        round_probs(t, j, kk)

                def slot(t, u, k):
                    ahead_part(t, u, k)
                    if k == 7:
                        out_of_psum(t, u)

                def out_of_psum(t, u):
                    ac.wait_ge(pv_done, after(t, u, (0, ALL), 7))
                    ac.wait_ge(norm_done, after(t, u, (0, ONCE), 0))
                    nc.scalar.activation(raw[:], acc_ps[:, :, 0:VC], ACT.Copy).then_inc(raw_done, 1)

                for sm, n in ((exp_done, 8), *[(cast_done[k], 1) for k in CAST_ACT], (qa_done, 2), (mrow_done, 2)):
                    ac.sem_inc(sm, n)
                for k in range(QUERY_SLOT, 8):
                    others(other, 0, -2, k)
                slots(ahead_part, 0, (-1,))
                with ac.Fori(0, B * H // 4) as t:
                    slots(slot, t, range(4))

            @block.gpsimd
            def _(pool):
                def part(t, j, k):
                    pj, pk = j - 1, k
                    if k in CAST_POOL:
                        wait_apart(pool, (exp_done, after(t, j, (0, ALL), k)), (pv_done, after(t, pj, (0, ALL), pk)))
                        nc.gpsimd.tensor_scalar(prob_hi[:, k, :], prob[:, k, :], 1.0, 1.0,
                                                ALU.mult, ALU.mult).then_inc(cast_done[k], 1)
                    if k in SUB_POOL:
                        pool.wait_ge(cast_done[k], after(t, j, (0, ONCE), 0))
                        nc.gpsimd.tensor_tensor(prob_lo[:, k, :], prob[:, k, :], prob_hi[:, k, :],
                                                ALU.subtract).then_inc(sub_done[k], 1)

                for sm in [cast_done[k] for k in CAST_POOL] + [sub_done[k] for k in SUB_POOL]:
                    pool.sem_inc(sm, 1)
                for k in range(AHEAD - 1):
                    part(0, 0, k)
                with pool.Fori(0, B * H // 4) as t:
                    slots(lambda t, u, k: part(t, *ahead(u, k, AHEAD - 1)), t, range(4))

            @block.vector
            def _(v):
                def other(t, j, item):
                    if item in ("q0", "q1"):
                        f = int(item[1])
                        v.wait_ge(qa_done, after(t, j, (0, HALVES), f))
                        at = slice(f * HALF, (f + 1) * HALF)
                        nc.vector.tensor_tensor(QB[0:LR, j % 4, at], x_ps[f][0:LR, :], QA[0:LR, j % 4, at],
                                                ALU.subtract).then_inc(ql_done, 1)
                    elif item in SIXTEEN:
                        v.wait_ge(smax_ready, after(t, j, (0, SIXTEEN), item))
                        nc.vector.tensor_reduce(part_max[:, item // 2, item % 2:item % 2 + 1], x_ps[item % 2][:],
                                                AX.X, ALU.max).then_inc(smax_done, 1)
                        if item == 15:
                            split_maxima(t, j)

                def split_maxima(t, j):
                    v.wait_ge(smax_done, after(t, j, (0, SIXTEEN), 15))
                    nc.vector.tensor_tensor(row_max[:], part_max[:, :, 0], part_max[:, :, 1], ALU.max).then_inc(split_done, 1)
                    v.wait_ge(mrow_ready, after(t, j - 1, (0, HALVES), 1))
                    v.wait_ge(split_done, after(t, j, (0, STEPS), 0))
                    nc.vector.tensor_copy(mz[:, :, LR], row_max[:]).then_inc(split_done, 1)
                    v.wait_ge(split_done, after(t, j, (0, STEPS), 1))
                    nc.vector.tensor_tensor(mz[:, :, LR + 1], row_max[:], mz[:, :, LR], ALU.subtract).then_inc(split_done, 1)

                def split_probs(t, j, k):
                    pj, pk = j - 1, k
                    if k in CAST_DVE:
                        v.wait_ge(exp_done, after(t, j, (0, ALL), k))
                        v.wait_ge(pv_done, after(t, pj, (0, ALL), pk))
                        nc.vector.tensor_copy(prob_hi[:, k, :], prob[:, k, :]).then_inc(cast_done[k], 1)
                    if k in SUB_DVE:
                        v.wait_ge(cast_done[k], after(t, j, (0, ONCE), 0))
                        nc.vector.tensor_tensor(prob_lo[:, k, :], prob[:, k, :], prob_hi[:, k, :],
                                                ALU.subtract).then_inc(sub_done[k], 1)

                def normalise(t, u):
                    b, h = place(t, u)
                    v.wait_ge(raw_done, after(t, u, (0, ONCE), 0))
                    nc.vector.reciprocal(rsum[:], raw[:, :, VC - 1]).then_inc(norm_steps, 1)
                    nc.vector.tensor_tensor(both[:], raw[:, :, 0:DC], raw[:, :, DC:2 * DC], ALU.add).then_inc(norm_steps, 1)
                    v.wait_ge(norm_steps, after(t, u, (0, HALVES), 1))
                    nc.vector.tensor_tensor(o_n[:, bass.ds(b * ST, ST), bass.ds(h * DC, DC)], both[:],
                                            rsum[:].unsqueeze(2).broadcast_to([P, ST, DC]), ALU.mult).then_inc(norm_done, 1)

                def ahead_part(t, u, k):
                    others(other, t, u, k, (0,))
                    j, kk = ahead(u, k, AHEAD - 1)
                    if j >= 0:
                        split_probs(t, j, kk)
                    if k == DIVIDE_SLOT and u >= 0:
                        normalise(t, u - 1)
                    others(other, t, u, k, (1, 2, 3))

                def slot(t, u, k):
                    ahead_part(t, u, k)

                for sm, n in ((smax_done, 16), (ql_done, 2), (split_done, 3), *[(sub_done[k], 1) for k in SUB_DVE],
                              *[(cast_done[k], 1) for k in CAST_DVE], (norm_done, 1)):
                    v.sem_inc(sm, n)
                nc.vector.memset(raw[:], 1.0).then_inc(raw_done, 1)
                for k in range(QUERY_SLOT, 8):
                    others(other, 0, -2, k)
                slots(ahead_part, 0, (-1,))
                with v.Fori(0, B * H // 4) as t:
                    slots(slot, t, range(4))
                normalise(B * H // 4 - 1, 3)
        inner.close()

        three = ExitStack()
        heads = sb(three, "heads", [P, 2, D])
        stage = sb(three, "stage", [P, 2, KD, P])
        projb = sb(three, "projb", [P, KD, D])
        gbias = sb(three, "gbias", [P, D])
        hs = sb(three, "hs", [P, 2, ST, D])
        hsT = sb(three, "hsT", [P, 2, KD, P])
        st3 = sb(three, "st3", [P, ST, 6])
        mv3 = sb(three, "mv3", [P, ST, 2])
        var3 = sb(three, "var3", [P, ST])
        rstd3 = sb(three, "rstd3", [P, ST])
        top = sb(three, "top", [P, ST])
        below = sb(three, "below", [P, ST, E])
        ex = sb(three, "ex", [P, ST, E])
        ranked = sb(three, "ranked", [P, ST, E])
        best = sb(three, "best", [P, ST])
        onehot = sb(three, "onehot", [P, ST, E], fp16)
        cum = sb(three, "cum", [P, ST + 1, E], fp16)
        picked = sb(three, "picked", [P, ST, E])
        pos = sb(three, "pos", [P, ST])
        start_of = sb(three, "start_of", [P, ST])
        kept = sb(three, "kept", [P, ST])
        slot_f = sb(three, "slot_f", [P, ST])
        moved = sb(three, "moved", [P, ST])
        total = sb(three, "total", [P, ST])
        recip = sb(three, "recip", [P, ST])
        to_slot = sb(three, "to_slot", [P, 2, ST], u32)
        a_ps = [ps(three, f"a_ps{n}", [P, HALF]) for n in range(2)]
        tr_ps = [ps(three, f"tr_ps{n}", [P, KD, P]) for n in range(2)]
        lg_ps = ps(three, "lg_ps", [P, ST, E])
        oT_ps = [ps(three, f"oT_ps{n}", [P, KD, P]) for n in range(2)]
        pos_ps = ps(three, "pos_ps", [P, ST, E])

        cum_zero = sem("cum_zero")
        biased = sem("biased")
        gbias_done = sem("gbias_done")
        scaled = sem("scaled")
        staged = sem("staged")
        fetched = sem("fetched")
        o_turned = sem("o_turned")
        projected = sem("projected")
        x1_done = sem("x1_done")
        stat3 = sem("stat3")
        var3_done = sem("var3_done")
        rstd3_done = sem("rstd3_done")
        centred = sem("centred")
        modulated = sem("modulated")
        turned = sem("turned")
        turned_out = sem("turned_out")
        logits = sem("logits")
        exps3 = sem("exps3")
        route = sem("route")
        pos_ready = sem("pos_ready")
        scattered = [sem(f"scattered{n}") for n in range(2)]
        rows_free = sem("rows_free")
        NROUTE = 27
        KR = tuple(range(NROUTE))

        def upto(t, u, n, k):
            return 2 * n * t + ((u + 1) * n + k + 1)

        with nc.Block() as block:
            @block.sync
            def _(sp):
                sp.sem_inc(rows_free, 2)
                with sp.Fori(0, B // 2) as t:
                    for u in range(2):
                        sp.wait_ge(scattered[u], 16 * ST * (t + 1))
                        sp.sem_inc(rows_free, 1)

            @block.scalar
            def _(ac):
                def fetch(t, u, n):
                    ac.wait_ge(o_turned, upto(t, u, ST, n - 2))
                    nc.scalar.activation(heads[:, n % 2, :], o_n[:, bass.ds((2 * t + u) * ST + n, 1), :].rearrange("p a d -> p (a d)"),
                                         ACT.Copy).then_inc(fetched, 1)

                for sm, n in ((staged, ST), (turned_out, ST), (exps3, 1), (fetched, ST)):
                    ac.sem_inc(sm, n)
                with ac.Fori(0, B // 2) as t:
                    for u in range(2):
                        for n in range(2 * ST):
                            if n == 0:
                                fetch(t, u, 0)
                            if n < ST:
                                if n + 1 < ST:
                                    fetch(t, u, n + 1)
                                ac.wait_ge(projected, upto(t, u, ST, n - 2))
                                ac.wait_ge(o_turned, upto(t, u, ST, n))
                                nc.scalar.activation(stage[:, n % 2, :, :], oT_ps[n % 2][:],
                                                     ACT.Copy).then_inc(staged, 1)
                            else:
                                m = n - ST
                                ac.wait_ge(turned, upto(t, u, ST, m))
                                nc.scalar.activation(hsT[:, m % 2, :, :], tr_ps[m % 2][:], ACT.Copy).then_inc(turned_out, 1)
                        ac.wait_ge(route, upto(t, u, NROUTE, 1))
                        nc.scalar.activation(ex[:], below[:], ACT.Exp).then_inc(exps3, 1)

            @block.gpsimd
            def _(pool):
                for b in range(B):
                    if b:
                        pool.wait_ge(biased, b)
                    nc.gpsimd.tensor_tensor(gbias[:], attn_bias[:], mod[:, b, GA, :], ALU.mult).then_inc(gbias_done, 1)
                    pool.wait_ge(gbias_done, b + 1)
                    nc.gpsimd.tensor_tensor(x1[:, b * ST:(b + 1) * ST, :], x1[:, b * ST:(b + 1) * ST, :],
                                            gbias[:].unsqueeze(1).broadcast_to([P, ST, D]), ALU.add).then_inc(biased, 1)
                for sm, n in ((rstd3_done, 2), (modulated, 2 * ST)):
                    pool.sem_inc(sm, n)
                with pool.Fori(0, B // 2) as t:
                    for u in range(2):
                        for g in range(2):
                            pool.wait_ge(var3_done, upto(t, u, 2, g))
                            nc.gpsimd.tensor_tensor(rstd3[:, 4 * g:4 * g + 4], var3[:, 4 * g:4 * g + 4],
                                                    minus_half[:, 0:4], ALU.pow).then_inc(rstd3_done, 1)
                            for n in range(4 * g, 4 * g + 4):
                                wait_apart(pool, (centred, upto(t, u, ST, n)))
                                nc.gpsimd.tensor_tensor(hs[:, u, n, :], hs[:, u, n, :],
                                                        mod[:, bass.ds(2 * t + u, 1), CB, :].rearrange("p a d -> p (a d)"),
                                                        ALU.mult).then_inc(modulated, 1)
                                wait_apart(pool, (modulated, upto(t, u, 2 * ST, 2 * n)))
                                nc.gpsimd.tensor_tensor(hs[:, u, n, :], hs[:, u, n, :],
                                                        mod[:, bass.ds(2 * t + u, 1), SB_, :].rearrange("p a d -> p (a d)"),
                                                        ALU.add).then_inc(modulated, 1)
                        pool.wait_ge(zeroed, 16 * ((SLOTS + P) // (7 * P)))
                        pool.wait_ge(route, upto(t, u, NROUTE, NROUTE - 1))
                        wait_apart(pool, (modulated, upto(t, u, 2 * ST, 2 * ST - 1)))
                        for n in range(ST):
                            nc.gpsimd.indirect_dma_start(
                                out=xbuf, out_offset=bass.IndirectOffsetOnAxis(ap=to_slot[:, u, n:n + 1], axis=0),
                                in_=hs[:, u, n, :], in_offset=None).then_inc(scattered[u], 16)
                for u in range(2):
                    pool.wait_ge(scattered[u], 16 * ST * B // 2)

            @block.vector
            def _(v):
                def centre(v, t, u, g):
                    v.wait_ge(rstd3_done, upto(t, u, 2, g))
                    for n in range(4 * g, 4 * g + 4):
                        nc.vector.tensor_scalar(hs[:, u, n, :],
                                                x1[:, bass.ds((2 * t + u) * ST + n, 1), :].rearrange("p a d -> p (a d)"),
                                                mv3[:, n, 0:1], rstd3[:, n:n + 1], ALU.subtract, ALU.mult).then_inc(centred, 1)

                def routing(v, t, u):
                    made = [0]

                    def step(ins, wait=True):
                        ins.then_inc(route, 1)
                        v.wait_ge(route, upto(t, u, NROUTE, made[0]))
                        made[0] += 1

                    def wide(ap):
                        return ap.unsqueeze(2).broadcast_to([P, ST, E])

                    rev_w = rev[:].unsqueeze(1).broadcast_to([P, ST, E])
                    first_w = first_slot[:].unsqueeze(1).broadcast_to([P, ST, E])
                    at = bass.ds((2 * t + u) * ST, ST)
                    V = nc.vector
                    v.wait_ge(logits, upto(t, u, ST, ST - 1))
                    step(V.tensor_reduce(top[:], lg_ps[:], AX.X, ALU.max))
                    v.wait_ge(exps3, upto(t, u, 1, -1))
                    step(V.tensor_tensor(below[:], lg_ps[:], wide(top[:]), ALU.subtract))
                    step(V.scalar_tensor_tensor(ranked[:], below[:], 0.0, rev_w, ALU.is_equal, ALU.mult))
                    step(V.tensor_reduce(best[:], ranked[:], AX.X, ALU.max))
                    v.wait_ge(pos_ready, upto(t, u, 1, -1))
                    step(V.tensor_tensor(onehot[:], rev_w, wide(best[:]), ALU.is_equal))
                    step(V.tensor_copy(cum[:, 0, :], cum[:, ST, :]))
                    for n in range(ST):
                        step(V.tensor_tensor(cum[:, n + 1, :], cum[:, n, :], onehot[:, n, :], ALU.add))
                    v.wait_ge(pos_ready, upto(t, u, 1, 0))
                    step(V.tensor_tensor(picked[:], pos_ps[:], onehot[:], ALU.mult))
                    step(V.tensor_reduce(pos[:], picked[:], AX.X, ALU.add))
                    step(V.tensor_tensor(ranked[:], first_w, onehot[:], ALU.mult))
                    step(V.tensor_reduce(start_of[:], ranked[:], AX.X, ALU.add))
                    step(V.tensor_scalar(kept[:], pos[:], float(CAP), None, ALU.is_le))
                    step(V.tensor_scalar(moved[:], pos[:], float(CAP), -1.0, ALU.min, ALU.add))
                    step(V.tensor_tensor(slot_f[:], moved[:], start_of[:], ALU.add))
                    step(V.tensor_copy(slot_of[:, at], slot_f[:]))
                    step(V.scalar_tensor_tensor(moved[:], slot_f[:], trash[:], kept[:], ALU.subtract, ALU.mult))
                    v.wait_ge(rows_free, 2 * t + (u + 1))
                    step(V.tensor_scalar(to_slot[:, u, :], moved[:], trash[:], None, ALU.add))
                    v.wait_ge(exps3, upto(t, u, 1, 0))
                    step(V.tensor_reduce(total[:], ex[:], AX.X, ALU.add))
                    step(V.reciprocal(recip[:], total[:]))
                    step(V.tensor_tensor(gate_of[:, at], recip[:], kept[:], ALU.mult))
                    assert made[0] == NROUTE

                nc.vector.memset(cum[:, ST, :], 0.0).then_inc(cum_zero, 1)
                v.wait_ge(cum_zero, 1)
                for sm, n in ((x1_done, ST), (stat3, 2 * ST), (var3_done, 2), (centred, ST), (route, NROUTE)):
                    v.sem_inc(sm, n)
                with v.Fori(0, B // 2) as t:
                    for u in range(2):
                        b = 2 * t + u
                        v.wait_ge(projected, upto(t, u, ST, -1))
                        nc.vector.tensor_tensor(projb[:], proj[:],
                                                mod[:, bass.ds(b, 1), GA, :].broadcast_to([P, KD, D]), ALU.mult).then_inc(scaled, 1)
                        v.wait_ge(rows_free, 2 * t + (u + 1))
                        v.wait_ge(biased, b + 1)
                        for g in range(2):
                            for n in range(4 * g, 4 * g + 4):
                                v.wait_ge(projected, upto(t, u, ST, n))
                                row = x1[:, bass.ds(b * ST + n, 1), :].rearrange("p a d -> p (a d)")
                                nc.vector.tensor_tensor(row, a_ps[n % 2][:, 0:D], row, ALU.add).then_inc(x1_done, 1)
                                wait_apart(v, (x1_done, upto(t, u, ST, n)))
                                nc.vector.bn_stats(st3[:, n, :], row).then_inc(stat3, 1)
                                wait_apart(v, (stat3, upto(t, u, 2 * ST, 2 * n)))
                                nc.vector.bn_aggr(mv3[:, n, :], st3[:, n, :]).then_inc(stat3, 1)
                            v.wait_ge(stat3, upto(t, u, 2 * ST, 8 * g + 7))
                            nc.vector.tensor_scalar(var3[:, 4 * g:4 * g + 4], mv3[:, 4 * g:4 * g + 4, 1], EPS, None,
                                                    ALU.add).then_inc(var3_done, 1)
                            if g == 1:
                                centre(v, t, u, 0)
                        centre(v, t, u, 1)
                        routing(v, t, u)

            @block.tensor
            def _(te):
                mm = nc.tensor.matmul

                def project(t, u, n):
                    te.wait_ge(staged, upto(t, u, ST, n))
                    if n == 0:
                        te.wait_ge(scaled, 2 * t + u + 1)
                    te.wait_ge(x1_done, upto(t, u, ST, n - 2))
                    for a in range(KD):
                        last = mm(a_ps[n % 2][:, 0:D], stage[:, n % 2, a, :], projb[:, a, :], start=a == 0, stop=a == KD - 1)
                    last.then_inc(projected, 1)

                def turn_heads(t, u, n):
                    te.wait_ge(staged, upto(t, u, ST, n - 2))
                    te.wait_ge(fetched, upto(t, u, ST, n))
                    for k in range(KD):
                        last = nc.tensor.transpose(oT_ps[n % 2][:, k, :],
                                                   heads[:, n % 2, k * P:(k + 1) * P], ident[:])
                    last.then_inc(o_turned, 1)

                def turn(t, u, n):
                    te.wait_ge(modulated, upto(t, u, 2 * ST, 2 * n + 1))
                    te.wait_ge(turned_out, upto(t, u, ST, n - 2))
                    for k in range(KD):
                        last = nc.tensor.transpose(tr_ps[n % 2][:, k, :], hs[:, u, n, k * P:(k + 1) * P], ident[:])
                    last.then_inc(turned, 1)

                def route_logits(t, u, n):
                    te.wait_ge(turned_out, upto(t, u, ST, n))
                    if n == 0:
                        te.wait_ge(route, upto(t, u, NROUTE, 1 - NROUTE))
                    for k in range(KD):
                        last = mm(lg_ps[:, n, :], hsT[:, n % 2, k, :], rwT[:, k, :], start=k == 0, stop=k == KD - 1)
                    last.then_inc(logits, 1)

                for sm, n in ((o_turned, ST), (projected, ST), (turned, ST), (logits, ST), (pos_ready, 1)):
                    te.sem_inc(sm, n)
                with te.Fori(0, B // 2) as t:
                    for u in range(2):
                        turn_heads(t, u, 0)
                        for n in range(ST):
                            if n + 1 < ST:
                                turn_heads(t, u, n + 1)
                            project(t, u, n)
                        for n in range(ST):
                            turn(t, u, n)
                            if n:
                                route_logits(t, u, n - 1)
                        route_logits(t, u, ST - 1)
                        te.wait_ge(route, upto(t, u, NROUTE, 4 + 1 + ST))
                        flat = pos_ps[:].rearrange("p t e -> p (t e)")
                        mm(flat, upto16[:], onehot[:].rearrange("p t e -> p (t e)"), start=True, stop=False)
                        mm(flat, ones16[:], cum[:, 0:ST, :].rearrange("p t e -> p (t e)"), start=False, stop=True).then_inc(pos_ready, 1)
        three.close()
        latents.close()

        four = ExitStack()
        w1f = sb(four, "w1f", [P, 2, KD, F])
        w2f = sb(four, "w2f", [P, 2, FT, D])
        w1h = sb(four, "w1h", [P, 2, KD, F], fp16)
        w1l = sb(four, "w1l", [P, 2, KD, F], fp16)
        w2h = sb(four, "w2h", [P, 2, FT, D], fp16)
        w2l = sb(four, "w2l", [P, 2, FT, D], fp16)
        b2w = sb(four, "b2w", [P, 2, D])
        b1c = sb(four, "b1c", [P, 2, FT])
        xb = sb(four, "xb", [P, 2, ET, D])
        xh = sb(four, "xh", [P, 2, KD * CAP], fp16)
        xl = sb(four, "xl", [P, 2, KD * CAP], fp16)
        act_f = sb(four, "act_f", [P, 2, CAP])
        act_h = sb(four, "act_h", [P, FT, CAP], fp16)
        act_l = sb(four, "act_l", [P, FT, CAP], fp16)
        yo = sb(four, "yo", [P, 2, ET, D])
        NW = CAP // 2
        xt_ps = [ps(four, f"xt_ps{n}", [P, HALF]) for n in range(2)]
        g_ps4 = [ps(four, f"g_ps{n}", [P, 2, HALF]) for n in range(2)]
        y_ps = [ps(four, f"y_ps{n}", [P, HALF]) for n in range(2)]

        w_in = [sem(f"w_in{n}") for n in range(2)]
        b2_in = [sem(f"b2_in{n}") for n in range(2)]
        split_w = sem("split_w")
        split_v = sem("split_v")
        xt_ready = sem("xt_ready")
        xh_done = sem("xh_done")
        xl_done = sem("xl_done")
        up_ready = sem("up_ready")
        gelu_done = sem("gelu_done")
        act_split = sem("act_split")
        y_ready = sem("y_ready")
        y_out = sem("y_out")
        y_stored = sem("y_stored")
        w1_e = w1.rearrange("e (k p) f -> e p k f", p=P)
        w2_e = w2.rearrange("e (f p) d -> e p f d", p=P)
        xb_e = xbuf[0:SLOTS, :].rearrange("(e s p) d -> e p s d", p=P, s=ET)
        yb_e = ybuf.rearrange("(e s p) d -> e p s d", p=P, s=ET)
        R3, E8, S6 = (0, 1, 2), tuple(range(FT)), tuple(range(ET))

        def past(t, u, events, k):
            return 2 * len(events) * t + ((u + 1) * len(events) + events.index(k) + 1)

        def experts(body, eng):
            with eng.Fori(0, E // 2 - 1) as t:
                for u in range(2):
                    body(t, u, True)
            body(E // 2 - 1, 0, True)
            body(E // 2 - 1, 1, False)

        with nc.Block() as block:
            @block.sync
            def _(sp):
                def load(e, u):
                    one_e = lambda a: (a[bass.ds(e, 1)] if not isinstance(e, int) else a[e:e + 1]).rearrange("a p k f -> p (a k) f")
                    sp.dma_start(xb[:, u, :, :], one_e(xb_e)).then_inc(w_in[u], 16)
                    sp.dma_start(w1f[:, u, :, :], one_e(w1_e)).then_inc(w_in[u], 16)
                    sp.dma_start(w2f[:, u, :, :], one_e(w2_e)).then_inc(w_in[u], 16)

                def load_b2(e, u):
                    row = b2[bass.ds(e, 1), :] if not isinstance(e, int) else b2[e:e + 1, :]
                    sp.dma_start(b2w[:, u, :], row.broadcast_to([P, D])).then_inc(b2_in[u], 16)

                def store(t, u):
                    e = 2 * t + u
                    sp.wait_ge(y_out, past(t, u, S6, 5))
                    dst = (yb_e[bass.ds(e, 1)] if not isinstance(e, int) else yb_e[e:e + 1]).rearrange("a p k f -> p (a k) f")
                    sp.dma_start(dst, yo[:, u, :, :]).then_inc(y_stored, 16)

                sp.sem_inc(y_stored, 1)
                for u in range(2):
                    load(u, u)
                    load_b2(u, u)
                with sp.Fori(0, E // 2 - 1) as t:
                    for u in range(2):
                        wait_apart(sp, (split_w, past(t, u, R3, 2)))
                        sp.wait_ge(split_v, past(t, u, (0, 1), 1))
                        sp.wait_ge(xt_ready, past(t, u, R3, 2))
                        load(2 * t + 2 + u, u)
                        store(t, u)
                        load_b2(2 * t + 2 + u, u)
                for u in range(2):
                    store(E // 2 - 1, u)
                sp.wait_ge(y_stored, 16 * E + 1)

            @block.gpsimd
            def _(pool):
                def split(t, u):
                    t_, u_ = (t, u) if u < 2 else (t + 1, u - 2)
                    wait_apart(pool, (y_ready, past(t, u - 2, S6, 5)), (w_in[u % 2], 48 * (t_ + 1)))
                    nc.gpsimd.tensor_scalar(w1h[:, u % 2], w1f[:, u % 2], 1.0, 1.0, ALU.mult, ALU.mult).then_inc(split_w, 1)
                    nc.gpsimd.tensor_scalar(w2h[:, u % 2], w2f[:, u % 2], 1.0, 1.0, ALU.mult, ALU.mult).then_inc(split_w, 1)
                    pool.wait_ge(split_w, past(t, u, R3, 1))
                    nc.gpsimd.tensor_tensor(w2l[:, u % 2], w2f[:, u % 2], w2h[:, u % 2], ALU.subtract).then_inc(split_w, 1)

                pool.sem_inc(split_w, 3)
                split(0, 0)

                def body(t, u, more):
                    if more:
                        split(t, u + 1)

                experts(body, pool)

            @block.scalar
            def _(ac):
                def rows_high(t, u):
                    for r in R3:
                        ac.wait_ge(xt_ready, past(t, u, R3, r))
                        nc.scalar.activation(xh[:, u % 2, r * HALF:(r + 1) * HALF], xt_ps[r % 2][:], ACT.Copy).then_inc(xh_done, 1)

                def body(t, u, more):
                    for f in E8:
                        ac.wait_ge(up_ready, past(t, u, E8, f))
                        if f == 0:
                            ac.wait_ge(split_v, past(t, u, (0, 1), 1))
                        pu, pf = (u, f - 2) if f >= 2 else (u - 1, f + 6)
                        ac.wait_ge(act_split, past(t, pu, tuple(range(2 * FT)), 2 * pf + 1))
                        nc.scalar.activation(act_f[:, f % 2, :].rearrange("p (n c) -> p n c", n=2), g_ps4[f % 2][:, :, 0:NW],
                                             ACT.Gelu, bias=b1c[:, u, f:f + 1]).then_inc(gelu_done, 1)
                    if more:
                        rows_high(t, u + 1)

                for sm, n in ((xh_done, 3), (gelu_done, FT)):
                    ac.sem_inc(sm, n)
                rows_high(0, 0)
                experts(body, ac)

            @block.vector
            def _(v):
                def prepare(t, u):
                    t_, u_ = (t, u) if u < 2 else (t + 1, u - 2)
                    e = 2 * t + u
                    v.wait_ge(split_w, past(t, u, R3, 0))
                    nc.vector.tensor_tensor(w1l[:, u % 2], w1f[:, u % 2], w1h[:, u % 2], ALU.subtract).then_inc(split_v, 1)
                    v.wait_ge(gelu_done, past(t, u - 2, E8, 7))
                    src = b1T[:, bass.ds(e, 1), :] if not isinstance(e, int) else b1T[:, e:e + 1, :]
                    nc.vector.tensor_copy(b1c[:, u % 2, :], src.rearrange("p a f -> p (a f)")).then_inc(split_v, 1)

                def rows_low(t, u):
                    for r in R3:
                        v.wait_ge(xh_done, past(t, u, R3, r))
                        at = slice(r * HALF, (r + 1) * HALF)
                        nc.vector.tensor_tensor(xl[:, u % 2, at], xt_ps[r % 2][:], xh[:, u % 2, at], ALU.subtract).then_inc(xl_done, 1)

                def body(t, u, more):
                    steps = tuple(range(2 * FT))
                    for f in E8:
                        v.wait_ge(gelu_done, past(t, u, E8, f))
                        nc.vector.tensor_copy(act_h[:, f, :], act_f[:, f % 2, :]).then_inc(act_split, 1)
                        v.wait_ge(act_split, past(t, u, steps, 2 * f))
                        nc.vector.tensor_tensor(act_l[:, f, :], act_f[:, f % 2, :], act_h[:, f, :], ALU.subtract).then_inc(act_split, 1)
                    if more:
                        rows_low(t, u + 1)
                        prepare(t, u + 1)
                    v.wait_ge(b2_in[u], 16 * (t + 1))
                    v.wait_ge(y_stored, 32 * t + 1)
                    for s in S6:
                        v.wait_ge(y_ready, past(t, u, S6, s))
                        nc.vector.tensor_tensor(yo[:, u, s, :], y_ps[s % 2][:, 0:D], b2w[:, u, :], ALU.add).then_inc(y_out, 1)

                for sm, n in ((split_v, 2), (xl_done, 3), (act_split, 2 * FT), (y_out, ET)):
                    v.sem_inc(sm, n)
                rows_low(0, 0)
                prepare(0, 0)
                experts(body, v)

            @block.tensor
            def _(te):
                mm = nc.tensor.matmul

                def turn(t, u):
                    t_, u_ = (t, u) if u < 2 else (t + 1, u - 2)
                    te.wait_ge(w_in[u % 2], 48 * (t_ + 1))
                    for r in R3:
                        pu, pr = (u, r - 2) if r >= 2 else (u - 1, r + 1 if r else 2)
                        te.wait_ge(xl_done, past(t, u, R3, r - 2) if r >= 2 else past(t, u - 1, R3, 2))
                        for n in range(4 * r, 4 * r + 4):
                            k, s = n // ET, n % ET
                            last = nc.tensor.transpose(xt_ps[r % 2][:, (n % 4) * P:(n % 4 + 1) * P],
                                                       xb[:, u % 2, s, k * P:(k + 1) * P], ident[:])
                        last.then_inc(xt_ready, 1)

                def body(t, u, more):
                    te.wait_ge(xl_done, past(t, u, R3, 2))
                    te.wait_ge(split_w, past(t, u, R3, 2))
                    te.wait_ge(split_v, past(t, u, (0, 1), 0))
                    for f in E8:
                        pu, pf = (u, f - 2) if f >= 2 else (u - 1, f + 6)
                        te.wait_ge(gelu_done, past(t, pu, E8, pf))
                        for w, x, i in ((w1h, xh, 0), (w1h, xl, 1), (w1l, xh, 2)):
                            for k in range(KD):
                                for n in range(2):
                                    last = mm(g_ps4[f % 2][:, n, 0:NW], w[:, u, k, f * P:(f + 1) * P],
                                              x[:, u, k * CAP + n * NW:k * CAP + (n + 1) * NW],
                                              start=i == 0 and k == 0, stop=i == 2 and k == KD - 1)
                        last.then_inc(up_ready, 1)
                    if more:
                        turn(t, u + 1)
                    for s in S6:
                        te.wait_ge(y_out, past(t, u, S6, s - 2) if s >= 2 else past(t, u - 1, S6, s + 4))
                        for f in E8:
                            if s == 0:
                                te.wait_ge(act_split, past(t, u, tuple(range(2 * FT)), 2 * f + 1))
                            for x, w, i in ((act_h, w2h, 0), (act_h, w2l, 1), (act_l, w2h, 2)):
                                last = mm(y_ps[s % 2][:, 0:D], x[:, f, s * P:(s + 1) * P], w[:, u, f, :],
                                          start=i == 0 and f == 0, stop=i == 2 and f == FT - 1)
                        last.then_inc(y_ready, 1)

                for sm, n in ((xt_ready, 3), (up_ready, FT), (y_ready, ET)):
                    te.sem_inc(sm, n)
                turn(0, 0)
                experts(body, te)
        four.close()

        five = ExitStack()
        yg = sb(five, "yg", [P, 2, ST, D])
        from_slot = sb(five, "from_slot", [P, 2, ST], u32)
        gate = sb(five, "gate", [P, 2, ST])
        picked_s = sem("picked_s")
        gathered = [sem(f"gathered{n}") for n in range(2)]
        gated = sem("gated")
        stored = [sem(f"stored{n}") for n in range(2)]
        with nc.Block() as block:
            @block.gpsimd
            def _(pool):
                with pool.Fori(0, B // 2) as t:
                    for u in range(2):
                        wait_apart(pool, (picked_s, 4 * t + 2 * u + 2), (stored[u], 16 * t + 1))
                        for n in range(ST):
                            nc.gpsimd.indirect_dma_start(
                                out=yg[:, u, n, :], out_offset=None, in_=ybuf,
                                in_offset=bass.IndirectOffsetOnAxis(ap=from_slot[:, u, n:n + 1], axis=0)).then_inc(gathered[u], 16)

            @block.vector
            def _(v):
                def pick(t, u):
                    at = bass.ds((2 * t + u) * ST, ST)
                    nc.vector.tensor_copy(from_slot[:, u, :], slot_of[:, at]).then_inc(picked_s, 1)
                    nc.vector.tensor_copy(gate[:, u, :], gate_of[:, at]).then_inc(picked_s, 1)

                with v.Fori(0, B // 2) as t:
                    for u in range(2):
                        pick(t, u)
                    for u in range(2):
                        v.wait_ge(gathered[u], 16 * ST * (t + 1))
                        v.wait_ge(picked_s, 4 * t + 4)
                        for n in range(ST):
                            b = 2 * t + u
                            nc.vector.scalar_tensor_tensor(yg[:, u, n, :], yg[:, u, n, :], gate[:, u, n:n + 1],
                                                           mod[:, bass.ds(b, 1), GB, :].rearrange("p a d -> p (a d)"),
                                                           ALU.mult, ALU.mult).then_inc(gated, 1)
                            v.wait_ge(gated, 4 * ST * t + (2 * ST * u + 2 * n + 1))
                            nc.vector.tensor_tensor(yg[:, u, n, :], yg[:, u, n, :],
                                                    x1[:, bass.ds(b * ST + n, 1), :].rearrange("p a d -> p (a d)"),
                                                    ALU.add).then_inc(gated, 1)

            @block.sync
            def _(sp):
                for u in range(2):
                    sp.sem_inc(stored[u], 1)
                with sp.Fori(0, B // 2) as t:
                    for u in range(2):
                        sp.wait_ge(gated, 4 * ST * t + 2 * ST * (u + 1))
                        sp.dma_start(out_tiles[:, bass.ds((2 * t + u) * ST, ST), :], yg[:, u, :, :]).then_inc(stored[u], 16)
                for u in range(2):
                    sp.wait_ge(stored[u], 16 * (B // 2) + 1)
        five.close()


NAMES = ["L0_attn_" + n for n in ("h_t", "W_DQ", "b_DQ", "W_UQ", "b_UQ", "W_DKV", "b_DKV", "W_UK", "b_UK", "W_UV",
                                  "b_UV", "W_QR", "b_QR", "W_KR", "b_KR", "W_O", "b_O")]
NAMES += ["L0_ffn_router_w", "L0_ffn_w1", "L0_ffn_b1", "L0_ffn_w2", "L0_ffn_b2", "L0_c", "L0_wmod"]


def kernel(**inputs):
    import concourse.bacc as bacc
    from concourse.bass_utils import run_bass_kernel_spmd

    nc = bacc.Bacc("TRN2", target_bir_lowering=False, num_devices=1)
    arrays, args = {}, []
    for name in NAMES:
        a = np.ascontiguousarray(inputs[name])
        arrays["in_" + name] = a
        args.append(nc.dram_tensor("in_" + name, a.shape, mybir.dt.from_np(a.dtype), kind="ExternalInput").ap())
    result = nc.dram_tensor("out_0", (B, S, D), fp32, kind="ExternalOutput").ap()
    adaln_block(nc, *args, result)
    r = run_bass_kernel_spmd(nc, [arrays], core_ids=[0])
    return r.results[0]["out_0"]
```
